# Optimizing a Trainium2 kernel written in Bass

```python
import numpy as np
import jax
import jax.numpy as jnp

def _softmax(x, axis=-1):
    return jax.nn.softmax(x, axis=axis)

def _gelu(x):
    return jax.nn.gelu(x, approximate=True)

def _silu(x):
    return jax.nn.silu(x)

def _sigmoid(x):
    return jax.nn.sigmoid(x)

def _layernorm(x, axis=-1, eps=1e-05):
    m = jnp.mean(x, axis=axis, keepdims=True)
    v = jnp.var(x, axis=axis, keepdims=True)
    return (x - m) / jnp.sqrt(v + eps)

def _scatter_add(tgt, idx, src, axis=0):
    return tgt.at[idx].add(src)

def _segment_sum(src, seg, n):
    return jax.ops.segment_sum(src, seg, n)
kernel_name = 'mk_adj_preln_d2_adj_r2_09d77f'

def setup_inputs(seed: int=0):
    np.random.seed(seed)
    _w = jnp.asarray

    def _rec_inputs():
        import jax
        import jax.numpy as jnp
        _gk = jax.random.key(seed)
        x = -0.0002928 + 1 * jax.random.normal(jax.random.fold_in(_gk, 1), (32, 256, 128), jnp.float32)
        _a = jax.random.bernoulli(jax.random.fold_in(_gk, 2), 0.015625, (256, 256))
        _a = jnp.logical_or(_a, jnp.swapaxes(_a, -1, -2))
        _a = jnp.logical_or(_a, jnp.eye(256, dtype=bool))
        _af = _a.astype(jnp.float32)
        adj = _af
        return (x, adj)
    x, adj = _rec_inputs()

    def _L0_gnn_setup():
        import jax, jax.numpy as jnp
        import numpy as np
        ALPHA = 0.2
        key = jax.random.key(seed)
        k1, k2, k3, k4 = jax.random.split(key, 4)
        B, N, Fin, Fout = (8, 1024, 128, 128)
        h = jax.random.normal(k1, (B, N, Fin), dtype=jnp.float32)
        adj = jax.random.randint(k2, (N, N), 0, 2).astype(jnp.float32)
        adj = jnp.maximum(adj, jnp.eye(N, dtype=jnp.float32))

        def xavier(k, shape, gain=1.414):
            fan_in, fan_out = (shape[0], shape[1])
            a = gain * np.sqrt(6.0 / (fan_in + fan_out))
            return jax.random.uniform(k, shape, dtype=jnp.float32, minval=-a, maxval=a)
        W = xavier(k3, (Fin, Fout))
        a = xavier(k4, (2 * Fout, 1))
        return {'h': h, 'adj_matrix': adj, 'W': W, 'a': a}
    _L0_gnn_all = _L0_gnn_setup()
    _L0_gnn_in = {k: v for k, v in _L0_gnn_all.items() if k in ('W', 'a')}
    del _L0_gnn_all

    def _L1_gnn_setup():
        import jax, jax.numpy as jnp
        import numpy as np
        B, T, D, H = (64, 1024, 128, 128)
        MAX_SKIP = 4

        def _lstm_last(Wih, Whh, bih, bhh, xs):
            N, _, Hd = xs.shape
            bias = bih + bhh

            def step(carry, x_t):
                h, c = carry
                g = x_t @ Wih.T + h @ Whh.T + bias
                i, f, gg, o = jnp.split(g, 4, axis=-1)
                c = jax.nn.sigmoid(f) * c + jax.nn.sigmoid(i) * jnp.tanh(gg)
                h = jax.nn.sigmoid(o) * jnp.tanh(c)
                return ((h, c), None)
            init = (jnp.zeros((N, Hd), xs.dtype), jnp.zeros((N, Hd), xs.dtype))
            (h_last, _), _ = jax.lax.scan(step, init, jnp.swapaxes(xs, 0, 1))
            return h_last
        key = jax.random.key(seed)
        ks = jax.random.split(key, 8)
        s = 0.05
        x = jax.random.normal(ks[0], (B, T, D), jnp.float32)
        adj = jax.random.uniform(ks[1], (T, T), jnp.float32) / T
        Wg0 = jax.random.normal(ks[2], (D, H), jnp.float32) * s
        bg0 = jnp.zeros((H,), jnp.float32)
        Wg1 = jax.random.normal(ks[3], (H, H), jnp.float32) * s
        bg1 = jnp.zeros((H,), jnp.float32)
        Wih = jax.random.normal(ks[4], (MAX_SKIP, 4 * H, H), jnp.float32) * s
        Whh = jax.random.normal(ks[5], (MAX_SKIP, 4 * H, H), jnp.float32) * s
        bih = jax.random.normal(ks[6], (MAX_SKIP, 4 * H), jnp.float32) * s
        bhh = jax.random.normal(ks[7], (MAX_SKIP, 4 * H), jnp.float32) * s
        return dict(x=x, adj=adj, Wg0=Wg0, bg0=bg0, Wg1=Wg1, bg1=bg1, Wih=Wih, Whh=Whh, bih=bih, bhh=bhh)
    _L1_gnn_all = _L1_gnn_setup()
    _L1_gnn_in = {k: v for k, v in _L1_gnn_all.items() if k in ('Wg0', 'bg0', 'Wg1', 'bg1', 'Wih', 'Whh', 'bih', 'bhh')}
    del _L1_gnn_all
    return {'x': x, 'adj': adj, 'L0_gnn_W': _L0_gnn_in['W'], 'L0_gnn_a': _L0_gnn_in['a'], 'L1_gnn_Wg0': _L1_gnn_in['Wg0'], 'L1_gnn_bg0': _L1_gnn_in['bg0'], 'L1_gnn_Wg1': _L1_gnn_in['Wg1'], 'L1_gnn_bg1': _L1_gnn_in['bg1'], 'L1_gnn_Wih': _L1_gnn_in['Wih'], 'L1_gnn_Whh': _L1_gnn_in['Whh'], 'L1_gnn_bih': _L1_gnn_in['bih'], 'L1_gnn_bhh': _L1_gnn_in['bhh']}

def reference(x, adj, L0_gnn_W, L0_gnn_a, L1_gnn_Wg0, L1_gnn_bg0, L1_gnn_Wg1, L1_gnn_bg1, L1_gnn_Wih, L1_gnn_Whh, L1_gnn_bih, L1_gnn_bhh):
    import jax
    import jax.numpy as jnp

    def _L0_gnn_ref(h, adj_matrix, W, a):
        import jax, jax.numpy as jnp
        import numpy as np
        ALPHA = 0.2
        Fout = W.shape[1]
        Wh = jnp.einsum('bnf,fo->bno', h, W)
        a1, a2 = (a[:Fout, 0], a[Fout:, 0])
        s1 = Wh @ a1
        s2 = Wh @ a2
        e = s1[:, :, None] + s2[:, None, :]
        e = jnp.where(e >= 0, e, ALPHA * e)
        e = jnp.where(adj_matrix[None] == 0, -jnp.inf, e)
        attention = jax.nn.softmax(e, axis=-1)
        h_prime = jnp.einsum('bij,bjo->bio', attention, Wh)
        return h_prime

    def _L1_gnn_ref(x, adj, Wg0, bg0, Wg1, bg1, Wih, Whh, bih, bhh):
        import jax, jax.numpy as jnp
        import numpy as np
        B, T, D, H = (64, 1024, 128, 128)
        MAX_SKIP = 4

        def _lstm_last(Wih, Whh, bih, bhh, xs):
            N, _, Hd = xs.shape
            bias = bih + bhh

            def step(carry, x_t):
                h, c = carry
                g = x_t @ Wih.T + h @ Whh.T + bias
                i, f, gg, o = jnp.split(g, 4, axis=-1)
                c = jax.nn.sigmoid(f) * c + jax.nn.sigmoid(i) * jnp.tanh(gg)
                h = jax.nn.sigmoid(o) * jnp.tanh(c)
                return ((h, c), None)
            init = (jnp.zeros((N, Hd), xs.dtype), jnp.zeros((N, Hd), xs.dtype))
            (h_last, _), _ = jax.lax.scan(step, init, jnp.swapaxes(xs, 0, 1))
            return h_last
        h = jax.nn.relu(jnp.einsum('ts,bsh->bth', adj, x @ Wg0 + bg0))
        h = jax.nn.relu(jnp.einsum('ts,bsh->bth', adj, h @ Wg1 + bg1))
        Bv, Tv, Hd = h.shape
        for p in range(1, MAX_SKIP + 1):
            nw = Tv // p
            wins = h[:, :nw * p, :].reshape(Bv * nw, p, Hd)
            last = _lstm_last(Wih[p - 1], Whh[p - 1], bih[p - 1], bhh[p - 1], wins)
            idx = jnp.arange(nw) * p + (p - 1)
            h = h.at[:, idx, :].set(last.reshape(Bv, nw, Hd))
        return h
    h = jnp.maximum(_layernorm(x, axis=-1), 0.0)
    x = x + _L0_gnn_ref(h, adj, L0_gnn_W, L0_gnn_a)
    h = jnp.maximum(_layernorm(x, axis=-1), 0.0)
    x = x + _L1_gnn_ref(h, adj, L1_gnn_Wg0, L1_gnn_bg0, L1_gnn_Wg1, L1_gnn_bg1, L1_gnn_Wih, L1_gnn_Whh, L1_gnn_bih, L1_gnn_bhh)
    return x

_drawn_inputs = setup_inputs


def setup_inputs(seed=0):
    import zlib

    import numpy as np

    out = dict(_drawn_inputs(seed))
    spreads = {'L1_gnn_bg0': (0.0, 0.1), 'L1_gnn_bg1': (0.0, 0.289)}
    factors = {'L1_gnn_Whh': 8.0, 'L1_gnn_bih': 3.65, 'L1_gnn_bhh': 3.596}
    for name, (base, spread) in spreads.items():
        noise = np.random.default_rng([zlib.crc32(name.encode()), seed]).standard_normal(out[name].shape)
        drawn = base * np.exp(spread * noise) if base else spread * noise
        out[name] = jnp.asarray(drawn.astype(out[name].dtype))
    for name, factor in factors.items():
        out[name] = (out[name] * factor).astype(out[name].dtype)
    return out
```

```python
import concourse.bass as bass
from concourse import mybir
from contextlib import ExitStack


def preln_gat_gcn_lstm_kernel(
    nc: bass.Bass,
    x: bass.AP,
    adj: bass.AP,
    adj_t: bass.AP,
    w_gat: bass.AP,
    w_gat_t: bass.AP,
    a_gat: bass.AP,
    w_gcn0: bass.AP,
    b_gcn0: bass.AP,
    w_gcn1: bass.AP,
    b_gcn1: bass.AP,
    w_ih_t: bass.AP,
    w_hh_t: bass.AP,
    b_ih_t: bass.AP,
    b_hh_t: bass.AP,
    out: bass.AP,
):
    fp32 = mybir.dt.float32
    fp32r = mybir.dt.float32r
    ALU = mybir.AluOpType
    ACT = mybir.ActivationFunctionType

    B, N, D = x.shape
    P = 128
    assert D == P and N == 2 * P
    TILES = B * N // P
    PAIRS = B // 2
    NODES = B * N
    QUARTER = TILES // 4
    PN = 2 * N
    EPS = 1e-5
    SLOPE = 0.2
    MASKED = -1e30
    SKIPS = 4
    GATES = 4
    I, F, G, O = range(GATES)

    x_v = x.rearrange("b (u p) f -> p (b u) f", p=P)
    out_v = out.rearrange("b (u p) f -> p (b u) f", p=P)

    ctx = ExitStack()
    with ctx:
        def sb(name, shape, dt=fp32):
            return ctx.enter_context(nc.sbuf_tensor(name, shape, dt))

        def sem(name):
            return ctx.enter_context(nc.semaphore(name))

        xs = sb("xs", [P, TILES, D])
        h_hi = sb("h_hi", [P, NODES], fp32r)
        h_lo = sb("h_lo", [P, NODES], fp32r)
        wl_hi = sb("wl_hi", [P, 2, SKIPS, GATES * D], fp32r)
        wl_lo = sb("wl_lo", [P, 2, SKIPS, GATES * D], fp32r)
        work = sb("work", [P, 8192])
        s_hi = sb("s_hi", [P, 4, 512], fp32r)
        s_lo = sb("s_lo", [P, 4, 512], fp32r)
        wh = sb("wh", [P, 2, 4, D + 2])
        adj_neg = sb("adj_neg", [P, 2, N])
        adjT_hi = sb("adjT_hi", [P, 2, N], fp32r)
        adjT_lo = sb("adjT_lo", [P, 2, N], fp32r)
        wext = sb("wext", [P, D + 1])
        wa2 = sb("wa2", [P, P])
        wt = sb("wt", [P, D])
        a12 = sb("a12", [P, 2])
        wg_raw = sb("wg_raw", [P, 2, D])
        wg_hi = sb("wg_hi", [P, 2, D], fp32r)
        wg_lo = sb("wg_lo", [P, 2, D], fp32r)
        brow = sb("brow", [64, 2, 512], fp32r)
        ones64 = sb("ones64", [64, P], fp32r)
        ident = sb("ident", [P, P])
        bl_raw = sb("bl_raw", [P, 2, SKIPS * GATES])
        bl = sb("bl", [P, SKIPS * GATES])
        stats = sb("stats", [P, 2, TILES, 6])
        mean = sb("mean", [P, 2, TILES])
        rstd = sb("rstd", [P, 2, TILES])
        ln_a = sb("ln_a", [P, TILES])
        ln_b = sb("ln_b", [P, TILES])
        ln_c = sb("ln_c", [P, TILES])
        half = sb("half", [P, TILES])
        m2 = sb("m2", [P, 2, 4])
        vtop = sb("vtop", [P, 4])
        vneg = sb("vneg", [P, 4])
        negm = sb("negm", [P, 4])
        ebias = sb("ebias", [P, 2, 4, 2])
        e_low = sb("e_low", [P, 4, N])
        rinv = sb("rinv", [P, 4])

        wraw = work[:, 0:4096].rearrange("p (w s g) -> p w s g", w=2, s=SKIPS)
        tt = work[:, 4096:6144].rearrange("p (q k j) -> p q k j", q=2, k=4)
        pT = work[:, 6144:7168].rearrange("p (k i) -> p k i", k=4)
        yn = work[:, 7168:7680].rearrange("p (k f) -> p k f", k=4)
        hT = work[:, 7680:8192]
        braw = work[0:64, 4096:5120].rearrange("p (l n) -> p l n", l=2)
        bhi = work[0:64, 5120:6144].rearrange("p (l n) -> p l n", l=2)
        araw = work[:, 6144:6656].rearrange("p (u n) -> p u n", u=2)
        araw2 = work[:, 6656:7168].rearrange("p (u n) -> p u n", u=2)
        lw = work[:, :].rearrange("p (q r n) -> p q r n", q=2, r=8)
        R_C, R_TC, R_IG, R_H = 4, 5, 6, 7

        ps = ctx.enter_context(nc.psum_tensor("ps", [P, 8, 512], fp32))
        psT = ps[:, 0, :]
        psW = ps[:, 1:3, 0:2 * (D + 1)]
        psS = ps[:, 3, :]
        psPT = ps[:, 4:6, :]
        psA = ps[:, 6:8, 0:2 * (D + 2)]

        x_in = [sem(f"x_in{c}") for c in range(4)]
        gat_w_in = sem("gat_w_in")
        adj_in = sem("adj_in")
        gcn_w_in = sem("gcn_w_in")
        lstm_w_in = sem("lstm_w_in")
        ident_ok = sem("ident_ok")
        pool_step = sem("pool_step")
        braw_zero = sem("braw_zero")
        consts_ok = sem("consts_ok")
        wa_ps = sem("wa_ps")
        wa_ok = sem("wa_ok")
        wl_ok = sem("wl_ok")
        stats_ok = sem("stats_ok")
        ln_ok = sem("ln_ok")
        dve_step = sem("dve_step")
        a_y = sem("a_y")
        a_T = sem("a_T")
        a_hT = sem("a_hT")
        a_W = sem("a_W")
        a_S = sem("a_S")
        a_wh = sem("a_wh")
        a_t = sem("a_t")
        a_bias = sem("a_bias")
        a_exp = sem("a_exp")
        a_P = sem("a_P")
        a_PT = sem("a_PT")
        a_pTa = sem("a_pTa")
        a_pTd = sem("a_pTd")
        a_att = sem("a_att")
        a_x1 = sem("a_x1")
        b_y = sem("b_y")
        b_mm = [sem(f"b_mm{s}") for s in range(5)]
        b_hi = [sem(f"b_hi{s}") for s in range(5)]
        b_lo = [sem(f"b_lo{s}") for s in range(5)]
        c_gate = [sem(f"c_gate{q}") for q in range(2)]
        c_act = [sem(f"c_act{q}") for q in range(2)]
        c_cell = [sem(f"c_cell{q}") for q in range(2)]
        c_h = [sem(f"c_h{q}") for q in range(2)]
        d_h = sem("d_h")
        d_T = sem("d_T")
        d_out = sem("d_out")
        stored = sem("stored")

        def ticks(eng, depth, unroll, body):
            lead = depth + 1 + (PAIRS - depth - 1) % unroll
            for t in range(lead):
                body(t, t % 2, lambda s, t=t: 0 <= t - s < PAIRS)
            if PAIRS > lead:
                with eng.Fori(0, (PAIRS - lead) // unroll) as it:
                    for k in range(unroll):
                        body(it * unroll + (lead + k), (lead + k) % 2, lambda s: True)
            for t in range(PAIRS, PAIRS + depth):
                body(t, t % 2, lambda s, t=t: 0 <= t - s < PAIRS)

        def lstm_rounds(eng, p, its, body):
            first = 0
            if p == LSTM[0][0]:
                body(0)
                first = 1
            with eng.Fori(first, its) as it:
                body(it)

        def pairs_two_by_two(eng, body):
            for par in range(2):
                body(par, par)
            with eng.Fori(1, PAIRS // 2) as it:
                for par in range(2):
                    body(it * 2 + par, par)

        def after(eng, s, n, least):
            if isinstance(n, int):
                if n > least:
                    eng.wait_ge(s, n)
            else:
                eng.wait_ge(s, n)

        LSTM = [(1, 2), (2, 4), (3, 4), (4, 8)]

        def lstm_shape(p, nb):
            return N // p, nb * (N // p), B // (2 * nb)

        def gates_of(p):
            return GATES * p - 1

        gate_base, act_base, h_base = {}, {}, {}
        g0 = a0 = h0 = 0
        for p, nb in LSTM:
            gate_base[p], act_base[p], h_base[p] = g0, a0, h0
            its = lstm_shape(p, nb)[2]
            g0 += its * gates_of(p)
            a0 += its * (gates_of(p) + p)
            h0 += its * p
        h_total = h0

        def window_cols(buf, p, nb, chunk, k):
            nw = N // p
            start = chunk * (nb * N)
            v = buf[:, bass.ds(start, nb * N)]
            if N % p == 0:
                return v.rearrange("f (w s) -> f w s", s=p)[:, :, k]
            v = v.rearrange("f (b t) -> f b t", b=nb)[:, :, k:k + (nw - 1) * p + 1:p]
            return v.rearrange("f b w -> f w b")

        def like_cols(buf2d, p, nb):
            nw, cols, _ = lstm_shape(p, nb)
            v = buf2d[:, 0:cols]
            if N % p == 0:
                return v
            return v.rearrange("f (w b) -> f w b", b=nb)

        block = ctx.enter_context(nc.Block())

        @block.sync
        def _(sp):
            step = TILES // 4
            for c in range(4):
                sp.dma_start(xs[:, c * step:(c + 1) * step, :],
                             x_v[:, c * step:(c + 1) * step, :]).then_inc(x_in[c], 16)
            sp.dma_start(wraw[:, 0], w_ih_t).then_inc(lstm_w_in, 16)
            sp.dma_start(wraw[:, 1], w_hh_t).then_inc(lstm_w_in, 16)

            with sp.Fori(0, PAIRS) as q:
                sp.wait_ge(d_out, q + 1)
                sp.dma_start(out_v[:, bass.ds(q * 4, 4), :], xs[:, bass.ds(q * 4, 4), :]).then_inc(stored, 16)
            sp.wait_ge(stored, 16 * PAIRS)

        @block.gpsimd
        def _(pool):
            n = 0

            def done(ins):
                nonlocal n
                n += 1
                ins.then_inc(pool_step, 1)
                pool.wait_ge(pool_step, n)

            done(nc.gpsimd.memset(ident[:, :], 0.0))
            nc.gpsimd.affine_select(out=ident[:, :], in_=ident[:, :], compare_op=ALU.not_equal, fill=1.0, base=0,
                                    pattern=[[-1, P]], channel_multiplier=1).then_inc(ident_ok, 1)
            done(nc.gpsimd.memset(half[:, :], -0.5))

            def norm_scale(which, lo, cnt, steps, count):
                st = stats[:, which, lo:lo + cnt, :]
                me, qe, mo, qo = st[:, :, 1], st[:, :, 2], st[:, :, 4], st[:, :, 5]
                a, b, c = (v[:, 0:cnt] for v in (ln_a, ln_b, ln_c))
                sub = [
                    lambda: nc.gpsimd.tensor_tensor(a, me, mo, ALU.add),
                    lambda: nc.gpsimd.tensor_scalar(mean[:, which, lo:lo + cnt], a, 0.5, 0.0, ALU.mult, ALU.add),
                    lambda: nc.gpsimd.tensor_tensor(b, me, mo, ALU.subtract),
                    lambda: nc.gpsimd.tensor_tensor(c, b, b, ALU.mult),
                    lambda: nc.gpsimd.tensor_scalar(c, c, 0.25, EPS, ALU.mult, ALU.add),
                    lambda: nc.gpsimd.tensor_tensor(b, qe, qo, ALU.add),
                    lambda: nc.gpsimd.tensor_scalar(b, b, 1.0 / D, 0.0, ALU.mult, ALU.add),
                    lambda: nc.gpsimd.tensor_tensor(a, b, c, ALU.add),
                    lambda: nc.gpsimd.tensor_tensor(rstd[:, which, lo:lo + cnt], a, half[:, 0:cnt], ALU.pow),
                ]
                for k, f in enumerate(sub[:-1]):
                    f().then_inc(pool_step, 1)
                    pool.wait_ge(pool_step, steps + (k + 1))
                sub[-1]().then_inc(ln_ok, 1)
                pool.wait_ge(ln_ok, count)
                return len(sub) - 1

            pool.wait_ge(stats_ok, TILES)
            n += norm_scale(0, 0, TILES, n, 1)

            pool.wait_ge(lstm_w_in, 32)
            for w in range(2):
                done(nc.gpsimd.tensor_copy(wl_hi[:, w], wraw[:, w]))
                nc.gpsimd.tensor_tensor(wl_lo[:, w], wraw[:, w], wl_hi[:, w].bitcast(fp32),
                                        ALU.subtract).then_inc(wl_ok, 1)

            for c in range(4):
                pool.wait_ge(stats_ok, TILES + (c + 1) * QUARTER)
                n += norm_scale(1, c * QUARTER, QUARTER, n, c + 2)

        @block.scalar
        def _(act):
            act.dma_start(wext[:, 0:D], w_gat).then_inc(gat_w_in, 16)
            act.dma_start(wt[:, :], w_gat_t).then_inc(gat_w_in, 16)
            act.dma_start(a12[:, :], a_gat).then_inc(gat_w_in, 16)
            act.dma_start(araw, adj.rearrange("(u p) n -> p u n", p=P)).then_inc(adj_in, 16)
            act.dma_start(araw2, adj_t.rearrange("(u p) n -> p u n", p=P)).then_inc(adj_in, 16)
            act.dma_start(wg_raw[:, 0], w_gcn0).then_inc(gcn_w_in, 16)
            act.dma_start(wg_raw[:, 1], w_gcn1).then_inc(gcn_w_in, 16)
            act.wait_ge(braw_zero, 1)
            for l, b in enumerate((b_gcn0, b_gcn1)):
                for r in (0, 32):
                    for k in range(4):
                        act.dma_start(braw[r:r + 1, l, k * D:(k + 1) * D],
                                      b.rearrange("(o f) -> o f", o=1)).then_inc(gcn_w_in, 16)
            act.dma_start(bl_raw[:, 0], b_ih_t.rearrange("f s g -> f (s g)")).then_inc(gcn_w_in, 16)
            act.dma_start(bl_raw[:, 1], b_hh_t.rearrange("f s g -> f (s g)")).then_inc(gcn_w_in, 16)

            def phase_a(t, par, live):
                if live(4):
                    act.wait_ge(a_PT, t - 3)
                    after(act, a_att, t - 4, 0)
                    nc.scalar.activation(pT[:, 0:2, :].rearrange("p k i -> p (k i)"), psPT[:, 0, :],
                                         ACT.Copy).then_inc(a_pTa, 1)
                if live(3):
                    pp = (par + 1) % 2
                    act.wait_ge(a_t, t - 2)
                    act.wait_ge(a_bias, t - 2)
                    after(act, a_P, t - 3, 0)
                    for k in range(4):
                        nc.scalar.activation(e_low[:, k], tt[:, pp, k], ACT.Exp, scale=SLOPE,
                                             bias=ebias[:, pp, k, 1:2])
                        ins = nc.scalar.activation(tt[:, pp, k], tt[:, pp, k], ACT.Exp,
                                                   bias=ebias[:, pp, k, 0:1])
                    ins.then_inc(a_exp, 1)
                if live(1):
                    act.wait_ge(a_T, t)
                    after(act, a_S, t - 1, 0)
                    nc.scalar.activation(hT, psT, ACT.Relu).then_inc(a_hT, 1)
                if live(2):
                    act.wait_ge(a_W, t - 1)
                    after(act, a_att, t - 3, 0)
                    nc.scalar.activation(
                        wh[:, par, :, 0:D + 1].rearrange("p (b u) f -> p b u f", b=2),
                        psW.rearrange("p b (u f) -> p b u f", u=2), ACT.Copy).then_inc(a_wh, 1)

            act.wait_ge(consts_ok, 1)
            ticks(act, 4, 2, phase_a)

            def phase_b(t, par, live):
                for s in (4, 3, 2, 1, 0):
                    if not live(s + 1):
                        continue
                    act.wait_ge(b_mm[s], t - s)
                    if s == 4:
                        dst = h_hi[:, bass.ds((t - 5) * PN, PN)]
                    else:
                        dst = s_hi[:, s, :]
                        after(act, b_mm[s + 1], t - s - 1, 0)
                    nc.scalar.activation(dst, ps[:, s, :], ACT.Copy if s in (1, 3) else ACT.Relu).then_inc(b_hi[s], 1)

            ticks(act, 5, 1, phase_b)

            act.wait_ge(wl_ok, 2)
            for p, nb in LSTM:
                nw, cols, its = lstm_shape(p, nb)
                def one(it):
                    for k in range(p):
                        for par in range(2):
                            gates = [I, G, O] if k == 0 else [I, G, F, O]
                            g_n = it * gates_of(p) + gate_base[p] + (0 if k == 0 else 3 + 4 * (k - 1))
                            h_n = it * p + h_base[p]
                            c_n = it * p + (h_base[p] + k + 1)
                            for j, g in enumerate(gates):
                                act.wait_ge(c_gate[par], g_n + (j + 1))
                                if k == 0 and j == 0:
                                    after(act, c_h[par], h_n, 0)
                                nc.scalar.activation(lw[:, par, g, 0:cols], ps[:, 4 * par + g, 0:cols],
                                                     ACT.Tanh if g == G else ACT.Sigmoid,
                                                     bias=bl[:, (p - 1) * GATES + g:(p - 1) * GATES + g + 1]
                                                     ).then_inc(c_act[par], 1)
                            act.wait_ge(c_cell[par], c_n)
                            nc.scalar.activation(lw[:, par, R_TC, 0:cols], lw[:, par, R_C, 0:cols],
                                                 ACT.Tanh).then_inc(c_act[par], 1)
                lstm_rounds(act, p, its, one)

        @block.vector
        def _(dve):
            n = 0

            def done(ins):
                nonlocal n
                n += 1
                ins.then_inc(dve_step, 1)
                dve.wait_ge(dve_step, n)

            nc.vector.memset(braw, 0.0).then_inc(braw_zero, 1)
            nc.vector.memset(ones64[:, :].bitcast(fp32), 1.0)
            nc.vector.memset(wh[:, :, :, D + 1:D + 2], 1.0)

            for c in range(4):
                dve.wait_ge(x_in[c], 16)
                with dve.Fori(c * (TILES // 4), (c + 1) * (TILES // 4)) as i:
                    nc.vector.bn_stats(stats[:, 0, bass.ds(i, 1), :].rearrange("p o s -> p (o s)"),
                                       xs[:, bass.ds(i, 1), :].rearrange("p o f -> p (o f)")).then_inc(stats_ok, 1)

            dve.wait_ge(adj_in, 32)
            nc.vector.tensor_scalar(adj_neg[:, :, :], araw, 0.0, MASKED, ALU.is_equal, ALU.mult)
            done(nc.vector.tensor_copy(adjT_hi[:, :, :], araw2))
            nc.vector.tensor_tensor(adjT_lo[:, :, :], araw2, adjT_hi[:, :, :].bitcast(fp32), ALU.subtract)
            dve.wait_ge(gcn_w_in, 16 * 20)
            done(nc.vector.tensor_copy(wg_hi[:, :, :], wg_raw[:, :, :]))
            nc.vector.tensor_tensor(wg_lo[:, :, :], wg_raw[:, :, :], wg_hi[:, :, :].bitcast(fp32), ALU.subtract)
            nc.vector.tensor_copy(brow[0:32], braw[0:32])
            done(nc.vector.tensor_copy(bhi[32:64].bitcast(fp32r), braw[32:64]))
            nc.vector.tensor_tensor(brow[32:64], braw[32:64], bhi[32:64], ALU.subtract)
            nc.vector.tensor_tensor(bl[:, :], bl_raw[:, 0], bl_raw[:, 1], ALU.add).then_inc(consts_ok, 1)
            dve.wait_ge(wa_ps, 1)
            nc.vector.tensor_copy(wext[:, D:D + 1], ps[:, 0, 0:1])
            nc.vector.tensor_copy(wa2[:, :], ps[:, 0, 1:2].to_broadcast([P, P])).then_inc(wa_ok, 1)
            dve.wait_ge(consts_ok, 1)

            def normalise(which, q, s_y, scores=None):
                for k in range(4):
                    i = q * 4 + k
                    if k == 3 and scores is not None:
                        dve.wait_ge(scores, q - 1)
                    ins = nc.vector.tensor_scalar(yn[:, k, :],
                                                  xs[:, bass.ds(i, 1), :].rearrange("p o f -> p (o f)"),
                                                  mean[:, which, bass.ds(i, 1)], rstd[:, which, bass.ds(i, 1)],
                                                  ALU.subtract, ALU.mult)
                ins.then_inc(s_y, 1)

            base = n

            def phase_a(t, par, live):
                pp = (par + 1) % 2
                if live(4):
                    dve.wait_ge(a_PT, t - 3)
                    after(dve, a_att, t - 4, 0)
                    nc.vector.tensor_copy(pT[:, 2:4, :].rearrange("p k i -> p (k i)"),
                                          psPT[:, 1, :]).then_inc(a_pTd, 1)
                if live(3):
                    a1 = wh[:, pp, :, D]
                    dve.wait_ge(a_wh, t - 2)
                    dve.wait_ge(a_t, t - 2)
                    nc.vector.tensor_tensor(vtop[:, :], m2[:, pp, :], a1, ALU.add).then_inc(dve_step, 1)
                    dve.wait_ge(dve_step, (t - 3) * 3 + (base + 1))
                    nc.vector.tensor_scalar(vneg[:, :], vtop[:, :], -SLOPE, None, ALU.mult).then_inc(dve_step, 1)
                    dve.wait_ge(dve_step, (t - 3) * 3 + (base + 2))
                    nc.vector.scalar_tensor_tensor(negm[:, :], vtop[:, :], -1.0, vneg[:, :], ALU.mult,
                                                   ALU.min).then_inc(dve_step, 1)
                    dve.wait_ge(dve_step, (t - 3) * 3 + (base + 3))
                    nc.vector.tensor_tensor(ebias[:, pp, :, 0], a1, negm[:, :], ALU.add)
                    nc.vector.scalar_tensor_tensor(ebias[:, pp, :, 1], a1, SLOPE, negm[:, :], ALU.mult,
                                                   ALU.add).then_inc(a_bias, 1)
                if live(0):
                    after(dve, a_T, t, 0)
                    normalise(0, t, a_y, a_S if live(2) else None)
                if live(2):
                    if not live(0):
                        dve.wait_ge(a_S, t - 1)
                    for k in range(4):
                        b, u = k // 2, k % 2
                        ins = nc.vector.tensor_tensor_reduce(
                            out=tt[:, par, k], in0=psS[:, b * N:(b + 1) * N], in1=adj_neg[:, u, :], scale=1.0,
                            scalar=-3e38, op0=ALU.add, op1=ALU.max, accum_out=m2[:, par, k:k + 1])
                    ins.then_inc(a_t, 1)
                if live(4):
                    dve.wait_ge(a_att, t - 3)
                    pa = psA.rearrange("p b (u f) -> p b u f", u=2)
                    nc.vector.reciprocal(rinv[:, :].rearrange("p (b u) -> p b u", b=2),
                                         pa[:, :, :, D + 1]).then_inc(a_x1, 1)
                    dve.wait_ge(a_x1, (t - 4) * 2 + 1)
                    for k in range(4):
                        xt = xs[:, bass.ds((t - 4) * 4 + k, 1), :].rearrange("p o f -> p (o f)")
                        ins = nc.vector.scalar_tensor_tensor(xt, pa[:, k // 2, k % 2, 0:D], rinv[:, k:k + 1], xt,
                                                             ALU.mult, ALU.add)
                    ins.then_inc(a_x1, 1)
                if live(3):
                    dve.wait_ge(a_exp, t - 2)
                    nc.vector.tensor_tensor(tt[:, pp], tt[:, pp], e_low[:, :, :], ALU.max).then_inc(a_P, 1)
                if live(4):
                    dve.wait_ge(a_x1, (t - 4) * 2 + 2)
                    for k in range(4):
                        nc.vector.bn_stats(stats[:, 1, bass.ds((t - 4) * 4 + k, 1), :].rearrange("p o s -> p (o s)"),
                                           xs[:, bass.ds((t - 4) * 4 + k, 1), :].rearrange("p o f -> p (o f)")
                                           ).then_inc(stats_ok, 1)

            dve.wait_ge(ln_ok, 1)
            ticks(dve, 4, 2, phase_a)

            def phase_b(t, par, live):
                for s in (4, 3, 2, 1, 0):
                    if not live(s + 1):
                        continue
                    dve.wait_ge(b_hi[s], t - s)
                    if s == 4:
                        hi = h_hi[:, bass.ds((t - 5) * PN, PN)]
                        dst = h_lo[:, bass.ds((t - 5) * PN, PN)]
                    else:
                        hi, dst = s_hi[:, s, :], s_lo[:, s, :]
                        after(dve, b_mm[s + 1], t - s - 1, 0)
                    if s in (1, 3):
                        ins = nc.vector.tensor_tensor(dst, ps[:, s, :], hi.bitcast(fp32), ALU.subtract)
                    else:
                        ins = nc.vector.scalar_tensor_tensor(dst, ps[:, s, :], 0.0, hi.bitcast(fp32), ALU.max,
                                                             ALU.subtract)
                    ins.then_inc(b_lo[s], 1)
                if live(0):
                    after(dve, b_mm[0], t, 0)
                    normalise(1, t, b_y)

            dve.wait_ge(a_T, PAIRS)
            dve.wait_ge(ln_ok, 5)
            ticks(dve, 5, 1, phase_b)

            steps = n + 3 * PAIRS
            for p, nb in LSTM:
                nw, cols, its = lstm_shape(p, nb)
                per = sum(2 * ((1 if k == 0 else 3) - 1 + 2) for k in range(p))
                def one(it):
                    s_n = 0
                    for k in range(p):
                        for par in range(2):
                            a_n = it * (gates_of(p) + p) + (act_base[p] + (0 if k == 0 else 4 + 5 * (k - 1)))
                            row = lambda r: lw[:, par, r, 0:cols]

                            def own(ins):
                                nonlocal s_n
                                s_n += 1
                                ins.then_inc(dve_step, 1)
                                dve.wait_ge(dve_step, it * per + (steps + s_n))

                            dve.wait_ge(c_act[par], a_n + 2)
                            if k == 0:
                                nc.vector.tensor_tensor(row(R_C), row(I), row(G), ALU.mult).then_inc(c_cell[par], 1)
                                dve.wait_ge(c_act[par], a_n + 4)
                            else:
                                own(nc.vector.tensor_tensor(row(R_IG), row(I), row(G), ALU.mult))
                                dve.wait_ge(c_act[par], a_n + 3)
                                own(nc.vector.tensor_tensor(row(R_C), row(F), row(R_C), ALU.mult))
                                nc.vector.tensor_tensor(row(R_C), row(R_C), row(R_IG), ALU.add
                                                        ).then_inc(c_cell[par], 1)
                                dve.wait_ge(c_act[par], a_n + 5)
                            own(nc.vector.tensor_tensor(row(R_H), row(O), row(R_TC), ALU.mult))
                            if k == p - 1:
                                hi = window_cols(h_hi, p, nb, it * 2 + par, k)
                                lo = window_cols(h_lo, p, nb, it * 2 + par, k)
                                src = like_cols(lw[:, par, R_H, :], p, nb)
                            else:
                                hi, lo = s_hi[:, par, 0:cols], s_lo[:, par, 0:cols]
                                src = row(R_H)
                            own(nc.vector.tensor_copy(hi, src))
                            nc.vector.tensor_tensor(lo, src, hi.bitcast(fp32), ALU.subtract).then_inc(c_h[par], 1)
                    assert s_n == per
                lstm_rounds(dve, p, its, one)
                steps += its * per

            dve.wait_ge(c_h[0], h_total)
            dve.wait_ge(c_h[1], h_total)

            def join(q, par):
                after(dve, d_T, q - 1, 0)
                nc.vector.tensor_tensor(lw[:, par, 0, :], h_hi[:, bass.ds(q * PN, PN)].bitcast(fp32),
                                        h_lo[:, bass.ds(q * PN, PN)].bitcast(fp32), ALU.add).then_inc(d_h, 1)

            def finish(q, par):
                dve.wait_ge(d_T, q + 1)
                xq = xs[:, bass.ds(q * 4, 4), :].rearrange("p k f -> p (k f)")
                nc.vector.tensor_tensor(xq, ps[:, par, :], xq, ALU.add).then_inc(d_out, 1)

            join(0, 0)
            join(1, 1)
            finish(0, 0)
            with dve.Fori(1, PAIRS // 2) as it:
                for par in range(2):
                    join(it * 2 + par, par)
                    finish(it * 2 + (par - 1), 1 - par)
            finish(PAIRS - 1, 1)

        @block.tensor
        def _(pe):
            pe.wait_ge(gat_w_in, 48)
            nc.tensor.matmul(ps[:, 0, 0:2], wt[:, :], a12[:, :], start=True, stop=True).then_inc(wa_ps, 1)
            pe.wait_ge(ident_ok, 1)
            pe.wait_ge(wa_ok, 1)

            def phase_a(t, par, live):
                if live(4):
                    pe.wait_ge(a_P, t - 3)
                    after(pe, a_pTa, t - 4, 0)
                    after(pe, a_pTd, t - 4, 0)
                    for k in range(4):
                        b, ui = k // 2, k % 2
                        for uj in range(2):
                            ins = nc.tensor.transpose(psPT[:, b, uj * N + ui * P:uj * N + (ui + 1) * P],
                                                      tt[:, par, k, uj * P:(uj + 1) * P], ident[:, :])
                    ins.then_inc(a_PT, 1)
                if live(1):
                    pe.wait_ge(a_y, t)
                    after(pe, a_hT, t - 1, 0)
                    for k in range(4):
                        ins = nc.tensor.transpose(psT[:, k * P:(k + 1) * P], yn[:, k, :], ident[:, :])
                    ins.then_inc(a_T, 1)
                if live(2):
                    pe.wait_ge(a_hT, t - 1)
                    after(pe, a_wh, t - 2, 0)
                    for k in range(4):
                        ins = nc.tensor.matmul(psW[:, k // 2, (k % 2) * (D + 1):(k % 2 + 1) * (D + 1)],
                                               hT[:, k * P:(k + 1) * P], wext[:, :], start=True, stop=True)
                    ins.then_inc(a_W, 1)
                    after(pe, a_t, t - 2, 0)
                    nc.tensor.matmul(psS, wa2[:, :], hT, start=True, stop=True).then_inc(a_S, 1)
                if live(4):
                    pe.wait_ge(a_pTa, t - 3)
                    pe.wait_ge(a_pTd, t - 3)
                    after(pe, a_x1, (t - 4) * 2, 0)
                    for b in range(2):
                        for ui in range(2):
                            for uj in range(2):
                                ins = nc.tensor.matmul(psA[:, b, ui * (D + 2):(ui + 1) * (D + 2)],
                                                       pT[:, 2 * b + uj, ui * P:(ui + 1) * P],
                                                       wh[:, par, 2 * b + uj, :],
                                                       start=(uj == 0), stop=(uj == 1))
                    ins.then_inc(a_att, 1)

            ticks(pe, 4, 2, phase_a)

            def product(dst, w, v, start, stop):
                for n_, (a, b) in enumerate(((w[0], v[0]), (w[1], v[0]), (w[0], v[1]))):
                    ins = nc.tensor.matmul(dst, a, b, start=start and n_ == 0, stop=stop and n_ == 2)
                return ins

            def parts(s):
                return s_hi[:, s, :], s_lo[:, s, :]

            def phase_b(t, par, live):
                for s in (4, 3, 2, 1, 0):
                    if not live(s + 1):
                        continue
                    after(pe, b_lo[s], t - s - 1, 0)
                    if s == 0:
                        pe.wait_ge(b_y, t)
                        for k in range(4):
                            ins = nc.tensor.transpose(ps[:, 0, k * P:(k + 1) * P], yn[:, k, :], ident[:, :])
                        ins.then_inc(b_mm[0], 1)
                        continue
                    pe.wait_ge(b_lo[s - 1], t - s)
                    hi, lo = parts(s - 1)
                    if s in (1, 3):
                        l = s // 2
                        nc.tensor.matmul(ps[:, s, :], ones64[:, :], brow[:, l, :], start=True, stop=False)
                        for k in range(4):
                            c = slice(k * P, (k + 1) * P)
                            ins = product(ps[:, s, c], (hi[:, c], lo[:, c]), (wg_hi[:, l, :], wg_lo[:, l, :]),
                                          False, k == 3)
                    else:
                        for b in range(2):
                            for u in range(2):
                                c = slice((2 * b + u) * P, (2 * b + u + 1) * P)
                                ins = product(ps[:, s, b * N:(b + 1) * N], (hi[:, c], lo[:, c]),
                                              (adjT_hi[:, u, :], adjT_lo[:, u, :]), u == 0, u == 1)
                    ins.then_inc(b_mm[s], 1)

            pe.wait_ge(consts_ok, 1)
            pe.wait_ge(a_x1, 2 * PAIRS)
            pe.wait_ge(a_hT, PAIRS)
            ticks(pe, 5, 1, phase_b)

            for s in range(5):
                pe.wait_ge(b_lo[s], PAIRS)
            pe.wait_ge(wl_ok, 2)
            for idx, (p, nb) in enumerate(LSTM):
                nw, cols, its = lstm_shape(p, nb)
                def one(it):
                    for k in range(p):
                        for par in range(2):
                            chunk = it * 2 + par
                            gates = [I, G, O] if k == 0 else [I, G, F, O]
                            if k == 0 and par == 0 and idx > 0:
                                pp, pnb = LSTM[idx - 1]
                                for q in range(2):
                                    pe.wait_ge(c_h[q], it * (pp * nb // pnb) + (h_base[pp] + pp * nb // pnb))
                            a_n = it * (gates_of(p) + p) + act_base[p] + (0 if k == 0 else 5 * k - 2)
                            after(pe, c_act[par], a_n, 0)
                            w = lambda m, g: (wl_hi[:, m, p - 1, g * D:(g + 1) * D], wl_lo[:, m, p - 1, g * D:(g + 1) * D])
                            v = (window_cols(h_hi, p, nb, chunk, k), window_cols(h_lo, p, nb, chunk, k))
                            dst = lambda g: like_cols(ps[:, 4 * par + g, :], p, nb)
                            for g in gates:
                                ins = product(dst(g), w(0, g), v, True, k == 0)
                                if k == 0:
                                    ins.then_inc(c_gate[par], 1)
                            if k > 0:
                                pe.wait_ge(c_h[par], it * p + (h_base[p] + k))
                                hv = (s_hi[:, par, 0:cols], s_lo[:, par, 0:cols])
                                for g in gates:
                                    product(ps[:, 4 * par + g, 0:cols], w(1, g), hv, False, True
                                            ).then_inc(c_gate[par], 1)
                lstm_rounds(pe, p, its, one)

            def turn(q, par):
                pe.wait_ge(d_h, q + 1)
                after(pe, d_out, q - 1, 0)
                for k in range(4):
                    ins = nc.tensor.transpose(ps[:, par, k * P:(k + 1) * P], lw[:, par, 0, k * P:(k + 1) * P],
                                              ident[:, :])
                ins.then_inc(d_T, 1)

            pairs_two_by_two(pe, turn)


def kernel(x, adj, L0_gnn_W, L0_gnn_a, L1_gnn_Wg0, L1_gnn_bg0, L1_gnn_Wg1, L1_gnn_bg1, L1_gnn_Wih, L1_gnn_Whh,
           L1_gnn_bih, L1_gnn_bhh):
    import numpy as np
    import concourse.bacc as bacc
    from concourse import mybir
    from concourse.bass_utils import run_bass_kernel_spmd

    x, adj, W = np.asarray(x), np.asarray(adj), np.asarray(L0_gnn_W)
    weight = lambda w: np.ascontiguousarray(np.asarray(w).transpose(2, 0, 1))
    bias = lambda b: np.ascontiguousarray(np.asarray(b).reshape(4, 4, 128).transpose(2, 0, 1))
    ins = {
        "x": x, "adj": adj, "adj_t": np.ascontiguousarray(adj.T), "w_gat": W, "w_gat_t": np.ascontiguousarray(W.T),
        "a_gat": np.ascontiguousarray(np.asarray(L0_gnn_a).reshape(2, 128).T), "w_gcn0": np.asarray(L1_gnn_Wg0), "b_gcn0": np.asarray(L1_gnn_bg0),
        "w_gcn1": np.asarray(L1_gnn_Wg1), "b_gcn1": np.asarray(L1_gnn_bg1), "w_ih_t": weight(L1_gnn_Wih),
        "w_hh_t": weight(L1_gnn_Whh), "b_ih_t": bias(L1_gnn_bih), "b_hh_t": bias(L1_gnn_bhh),
    }
    nc = bacc.Bacc("TRN2", target_bir_lowering=False, num_devices=1)
    arrays, args = {}, []
    for name, a in ins.items():
        arrays[f"in_{name}"] = a
        args.append(nc.dram_tensor(f"in_{name}", a.shape, mybir.dt.from_np(a.dtype), kind="ExternalInput").ap())
    args.append(nc.dram_tensor("result", x.shape, mybir.dt.from_np(x.dtype), kind="ExternalOutput").ap())
    preln_gat_gcn_lstm_kernel(nc, *args)
    r = run_bass_kernel_spmd(nc, [arrays], core_ids=[0])
    return r.results[0]["result"]
```

```python
import concourse.bass as bass
from concourse import mybir
from contextlib import ExitStack


def preln_gat_gcn_lstm_kernel(
    nc: bass.Bass,
    x: bass.AP,
    adj: bass.AP,
    adj_t: bass.AP,
    w_gat: bass.AP,
    w_gat_t: bass.AP,
    a_gat: bass.AP,
    w_gcn0: bass.AP,
    b_gcn0: bass.AP,
    w_gcn1: bass.AP,
    b_gcn1: bass.AP,
    w_ih_t: bass.AP,
    w_hh_t: bass.AP,
    b_ih_t: bass.AP,
    b_hh_t: bass.AP,
    out: bass.AP,
):
    fp32 = mybir.dt.float32
    fp32r = mybir.dt.float32r
    ALU = mybir.AluOpType
    ACT = mybir.ActivationFunctionType

    B, N, D = x.shape
    P = 128
    assert D == P and N == 2 * P
    TILES = B * N // P
    PAIRS = B // 2
    NODES = B * N
    QUARTER = TILES // 4
    PN = 2 * N
    EPS = 1e-5
    SLOPE = 0.2
    MASKED = -1e30
    SKIPS = 4
    GCN_LOADS = 10
    GATES = 4
    I, F, G, O = range(GATES)

    x_v = x.rearrange("b (u p) f -> p (b u) f", p=P)
    out_v = out.rearrange("b (u p) f -> p (b u) f", p=P)

    ctx = ExitStack()
    with ctx:
        def sb(name, shape, dt=fp32):
            return ctx.enter_context(nc.sbuf_tensor(name, shape, dt))

        def sem(name):
            return ctx.enter_context(nc.semaphore(name))

        xs = sb("xs", [P, TILES, D])
        wl_hi = sb("wl_hi", [P, 2, SKIPS, GATES * D], fp32r)
        wl_lo = sb("wl_lo", [P, 2, SKIPS, GATES * D], fp32r)
        work = sb("work", [P, 8192])
        s_hi = sb("s_hi", [P, 4, 512], fp32r)
        s_lo = sb("s_lo", [P, 4, 512], fp32r)
        v_norm = sb("v_norm", [P, 4, D])
        adj_raw = sb("adj_raw", [P, 2, N])
        adjT_raw = sb("adjT_raw", [P, 2, N])
        adj_neg = sb("adj_neg", [P, 2, N])
        adjT_hi = sb("adjT_hi", [P, 2, N], fp32r)
        adjT_lo = sb("adjT_lo", [P, 2, N], fp32r)
        wext = sb("wext", [P, D + 1])
        wa2 = sb("wa2", [P, P])
        wt = sb("wt", [P, D])
        a12 = sb("a12", [P, 2])
        wg_raw = sb("wg_raw", [P, 2, D])
        wg_hi = sb("wg_hi", [P, 2, D], fp32r)
        wg_lo = sb("wg_lo", [P, 2, D], fp32r)
        b_raw = sb("b_raw", [96, 2, D])
        b_full = sb("b_full", [96, 2, D])
        b0_parts = sb("b0_parts", [96, D], fp32r)
        b1_parts = sb("b1_parts", [64, 4, D], fp32r)
        rs_full = sb("rs_full", [P, N])
        rs_parts = sb("rs_parts", [96, N], fp32r)
        ones = sb("ones", [P, P], fp32r)
        ident = sb("ident", [P, P])
        ident_r = sb("ident_r", [P, P], fp32r)
        bl_raw = sb("bl_raw", [P, 2, SKIPS * GATES])
        bl = sb("bl", [P, SKIPS * GATES])
        stats = sb("stats", [P, 2, TILES, 6])
        shift = sb("shift", [P, 2, TILES])
        scale = sb("scale", [P, 2, TILES])
        ln_a = sb("ln_a", [P, TILES])
        ln_b = sb("ln_b", [P, TILES])
        ln_c = sb("ln_c", [P, TILES])
        half = sb("half", [P, TILES])
        m2 = sb("m2", [P, 3, 4])
        vtop = sb("vtop", [P, 4])
        vneg = sb("vneg", [P, 4])
        negm = sb("negm", [P, 4])
        ebias = sb("ebias", [P, 3, 4, 2])
        rinv = sb("rinv", [P, 4])

        with ExitStack() as early:
            def sb_early(name, shape):
                return early.enter_context(nc.sbuf_tensor(name, shape, fp32))

            hT = sb_early("hT", [P, 512])
            score = sb_early("score", [P, 3, 4, N])
            e_one = sb_early("e_one", [P, 4, N])
            e_low = sb_early("e_low", [P, 4, N])
            prob = sb_early("prob", [P, 4, N])
            pT = sb_early("pT", [P, 4, N])
            wh = sb_early("wh", [P, 3, 4, D + 2])
        h_hi = sb("h_hi", [P, NODES], fp32r)
        h_lo = sb("h_lo", [P, NODES], fp32r)

        wraw = work[:, 0:4096].rearrange("p (w s g) -> p w s g", w=2, s=SKIPS)
        lw = work[:, :].rearrange("p (q r n) -> p q r n", q=2, r=8)
        R_C, R_TC, R_IG, R_H = 4, 5, 6, 7

        ps = ctx.enter_context(nc.psum_tensor("ps", [P, 8, 512], fp32))
        psT = ps[:, 0, :]
        psW = ps[:, 1:3, 0:2 * (D + 1)]
        psS = ps[:, 3, :]
        psPT = ps[:, 4:6, :]
        psA = ps[:, 6:8, 0:2 * (D + 2)]

        x_in = [sem(f"x_in{c}") for c in range(4)]
        gat_w_in = sem("gat_w_in")
        adj_in = sem("adj_in")
        gcn_w_in = sem("gcn_w_in")
        lstm_w_in = sem("lstm_w_in")
        ident_ok = sem("ident_ok")
        pool_step = sem("pool_step")
        b_zero = sem("b_zero")
        ones_ok = sem("ones_ok")
        rs_ps = sem("rs_ps")
        rs_ok = sem("rs_ok")
        adjT_ok = sem("adjT_ok")
        b_ok = sem("b_ok")
        wa_ps = sem("wa_ps")
        wa_ok = sem("wa_ok")
        wl_ok = sem("wl_ok")
        stats_ok = sem("stats_ok")
        ln_ok = sem("ln_ok")
        dve_step = sem("dve_step")
        a_y = sem("a_y")
        a_T = sem("a_T")
        a_hT = sem("a_hT")
        a_W = sem("a_W")
        a_S = sem("a_S")
        a_wh = sem("a_wh")
        a_t = sem("a_t")
        a_bias = sem("a_bias")
        a_exp = sem("a_exp")
        a_P = sem("a_P")
        a_PT = sem("a_PT")
        a_pT = sem("a_pT")
        a_att = sem("a_att")
        a_x1 = sem("a_x1")
        b_v = sem("b_v")
        b_mm = [None] + [sem(f"b_mm{s}") for s in range(1, 5)]
        b_hi = [sem(f"b_hi{s}") for s in range(5)]
        b_lo = [sem(f"b_lo{s}") for s in range(5)]
        c_gate = [sem(f"c_gate{q}") for q in range(2)]
        c_act = [sem(f"c_act{q}") for q in range(2)]
        c_cell = [sem(f"c_cell{q}") for q in range(2)]
        c_h = [sem(f"c_h{q}") for q in range(2)]
        d_T = sem("d_T")
        d_out = sem("d_out")
        stored = sem("stored")

        def ticks(eng, depth, unroll, body):
            lead = depth + 1 + (PAIRS - depth - 1) % unroll
            for t in range(lead):
                body(t, t, lambda s, t=t: 0 <= t - s < PAIRS)
            if PAIRS > lead:
                with eng.Fori(0, (PAIRS - lead) // unroll) as it:
                    for k in range(unroll):
                        body(it * unroll + (lead + k), lead + k, lambda s: True)
            for t in range(PAIRS, PAIRS + depth):
                body(t, t, lambda s, t=t: 0 <= t - s < PAIRS)

        def lstm_rounds(eng, p, its, body):
            first = 0
            if p == LSTM[0][0]:
                body(0)
                first = 1
            with eng.Fori(first, its) as it:
                body(it)

        def after(eng, s, n, least):
            if isinstance(n, int):
                if n > least:
                    eng.wait_ge(s, n)
            else:
                eng.wait_ge(s, n)

        LSTM = [(1, 2), (2, 4), (3, 4), (4, 8)]

        def lstm_shape(p, nb):
            return N // p, nb * (N // p), B // (2 * nb)

        def gates_of(p):
            return GATES * p - 1

        gate_base, act_base, h_base = {}, {}, {}
        g0 = a0 = h0 = 0
        for p, nb in LSTM:
            gate_base[p], act_base[p], h_base[p] = g0, a0, h0
            its = lstm_shape(p, nb)[2]
            g0 += its * gates_of(p)
            a0 += its * (gates_of(p) + p)
            h0 += its * p
        h_total = h0

        def window_cols(buf, p, nb, chunk, k):
            nw = N // p
            start = chunk * (nb * N)
            v = buf[:, bass.ds(start, nb * N)]
            if N % p == 0:
                return v.rearrange("f (w s) -> f w s", s=p)[:, :, k]
            v = v.rearrange("f (b t) -> f b t", b=nb)[:, :, k:k + (nw - 1) * p + 1:p]
            return v.rearrange("f b w -> f w b")

        def like_cols(buf2d, p, nb):
            nw, cols, _ = lstm_shape(p, nb)
            v = buf2d[:, 0:cols]
            if N % p == 0:
                return v
            return v.rearrange("f (w b) -> f w b", b=nb)

        block = ctx.enter_context(nc.Block())

        @block.sync
        def _(sp):
            step = TILES // 4
            for c in range(4):
                sp.dma_start(xs[:, c * step:(c + 1) * step, :],
                             x_v[:, c * step:(c + 1) * step, :]).then_inc(x_in[c], 16)
            sp.dma_start(wraw[:, 0], w_ih_t).then_inc(lstm_w_in, 16)
            sp.dma_start(wraw[:, 1], w_hh_t).then_inc(lstm_w_in, 16)

            with sp.Fori(0, PAIRS) as q:
                sp.wait_ge(d_out, q + 1)
                sp.dma_start(out_v[:, bass.ds(q * 4, 4), :], xs[:, bass.ds(q * 4, 4), :]).then_inc(stored, 16)
            sp.wait_ge(stored, 16 * PAIRS)

        @block.gpsimd
        def _(pool):
            n = 0

            def done(ins):
                nonlocal n
                n += 1
                ins.then_inc(pool_step, 1)
                pool.wait_ge(pool_step, n)

            done(nc.gpsimd.memset(b_raw[:, :, :], 0.0))
            nc.gpsimd.nop().then_inc(b_zero, 1)
            done(nc.gpsimd.memset(ident[:, :], 0.0))
            nc.gpsimd.affine_select(out=ident[:, :], in_=ident[:, :], compare_op=ALU.not_equal, fill=1.0, base=0,
                                    pattern=[[-1, P]], channel_multiplier=1).then_inc(ident_ok, 1)
            nc.gpsimd.memset(wh[:, :, :, D + 1:D + 2], 1.0)
            nc.gpsimd.memset(ones[:, :].bitcast(fp32), 1.0).then_inc(ones_ok, 1)
            done(nc.gpsimd.memset(half[:, :], -0.5))

            def norm_scale(which, c):
                nonlocal n
                lo = c * QUARTER
                st = stats[:, which, lo:lo + QUARTER, :]
                me, qe, mo, qo = st[:, :, 1], st[:, :, 2], st[:, :, 4], st[:, :, 5]
                a, b, d = (v[:, 0:QUARTER] for v in (ln_a, ln_b, ln_c))
                sc, sh = scale[:, which, lo:lo + QUARTER], shift[:, which, lo:lo + QUARTER]
                done(nc.gpsimd.tensor_tensor(b, me, mo, ALU.subtract))
                done(nc.gpsimd.tensor_tensor(d, b, b, ALU.mult))
                done(nc.gpsimd.tensor_scalar(d, d, 0.25, EPS, ALU.mult, ALU.add))
                done(nc.gpsimd.tensor_tensor(b, qe, qo, ALU.add))
                done(nc.gpsimd.tensor_scalar(b, b, 1.0 / D, 0.0, ALU.mult, ALU.add))
                done(nc.gpsimd.tensor_tensor(a, b, d, ALU.add))
                done(nc.gpsimd.tensor_tensor(sc, a, half[:, 0:QUARTER], ALU.pow))
                done(nc.gpsimd.tensor_tensor(b, me, mo, ALU.add))
                done(nc.gpsimd.tensor_scalar(b, b, -0.5, 0.0, ALU.mult, ALU.add))
                nc.gpsimd.tensor_tensor(sh, b, sc, ALU.mult).then_inc(ln_ok, 1)
                pool.wait_ge(ln_ok, which * 4 + c + 1)

            for c in range(4):
                pool.wait_ge(stats_ok, (c + 1) * QUARTER)
                norm_scale(0, c)

            pool.wait_ge(adj_in, 32)
            done(nc.gpsimd.tensor_copy(adjT_hi[:, :, :], adjT_raw[:, :, :]))
            nc.gpsimd.tensor_tensor(adjT_lo[:, :, :], adjT_raw[:, :, :], adjT_hi[:, :, :].bitcast(fp32),
                                    ALU.subtract).then_inc(adjT_ok, 1)
            pool.wait_ge(gcn_w_in, GCN_LOADS * 16)
            done(nc.gpsimd.tensor_copy(wg_hi[:, :, :], wg_raw[:, :, :]))
            nc.gpsimd.tensor_tensor(wg_lo[:, :, :], wg_raw[:, :, :], wg_hi[:, :, :].bitcast(fp32), ALU.subtract)
            nc.gpsimd.tensor_copy(ident_r[:, :], ident[:, :])
            nc.gpsimd.tensor_tensor(bl[:, :], bl_raw[:, 0], bl_raw[:, 1], ALU.add)
            done(nc.gpsimd.tensor_copy(b_full[:, :, :].bitcast(fp32r), b_raw[:, :, :]))
            done(nc.gpsimd.tensor_copy(b0_parts[0:32], b_full[0:32, 0]))
            done(nc.gpsimd.tensor_tensor(b0_parts[32:64], b_raw[32:64, 0], b_full[32:64, 0], ALU.subtract))
            done(nc.gpsimd.tensor_copy(b0_parts[64:96], b_full[64:96, 0]))
            for k in range(4):
                done(nc.gpsimd.tensor_copy(b1_parts[0:32, k], b_full[0:32, 1]))
                done(nc.gpsimd.tensor_tensor(b1_parts[32:64, k], b_raw[32:64, 1], b_full[32:64, 1], ALU.subtract))
            nc.gpsimd.nop().then_inc(b_ok, 1)

            pool.wait_ge(lstm_w_in, 32)
            for w in range(2):
                done(nc.gpsimd.tensor_copy(wl_hi[:, w], wraw[:, w]))
                nc.gpsimd.tensor_tensor(wl_lo[:, w], wraw[:, w], wl_hi[:, w].bitcast(fp32),
                                        ALU.subtract).then_inc(wl_ok, 1)
                pool.wait_ge(wl_ok, w + 1)

            for c in range(4):
                pool.wait_ge(stats_ok, TILES + (c + 1) * QUARTER)
                norm_scale(1, c)

        @block.scalar
        def _(act):
            act.dma_start(wext[:, 0:D], w_gat).then_inc(gat_w_in, 16)
            act.dma_start(wt[:, :], w_gat_t).then_inc(gat_w_in, 16)
            act.dma_start(a12[:, :], a_gat).then_inc(gat_w_in, 16)
            act.dma_start(adj_raw[:, :, :], adj.rearrange("(u p) n -> p u n", p=P)).then_inc(adj_in, 16)
            act.dma_start(adjT_raw[:, :, :], adj_t.rearrange("(u p) n -> p u n", p=P)).then_inc(adj_in, 16)
            act.dma_start(wg_raw[:, 0], w_gcn0).then_inc(gcn_w_in, 16)
            act.dma_start(wg_raw[:, 1], w_gcn1).then_inc(gcn_w_in, 16)
            act.dma_start(bl_raw[:, 0], b_ih_t.rearrange("f s g -> f (s g)")).then_inc(gcn_w_in, 16)
            act.dma_start(bl_raw[:, 1], b_hh_t.rearrange("f s g -> f (s g)")).then_inc(gcn_w_in, 16)
            act.wait_ge(b_zero, 1)
            for l, b in enumerate((b_gcn0, b_gcn1)):
                for r in (0, 32, 64):
                    act.dma_start(b_raw[r:r + 1, l, :], b.rearrange("(o f) -> o f", o=1)).then_inc(gcn_w_in, 16)

            def normalise(which, q, s_v):
                for k in range(4):
                    i = q * 4 + k
                    ins = nc.scalar.activation(v_norm[:, k, :],
                                               xs[:, bass.ds(i, 1), :].rearrange("p o f -> p (o f)"), ACT.Relu,
                                               scale=scale[:, which, bass.ds(i, 1)],
                                               bias=shift[:, which, bass.ds(i, 1)])
                ins.then_inc(s_v, 1)

            def phase_a(t, ph, live):
                if live(1):
                    act.wait_ge(a_T, t)
                    after(act, a_S, t - 1, 0)
                    nc.scalar.activation(hT[:, :], psT, ACT.Copy).then_inc(a_hT, 1)
                if live(0):
                    if isinstance(t, int):
                        act.wait_ge(ln_ok, t * 4 // QUARTER + 1 if t < 6 else 4)
                    after(act, a_T, t, 0)
                    normalise(0, t, a_y)
                if live(2):
                    m = (ph - 2) % 3
                    act.wait_ge(a_bias, t - 1)
                    after(act, a_P, t - 2, 0)
                    for k in range(4):
                        nc.scalar.activation(e_low[:, k], score[:, m, k], ACT.Exp, scale=SLOPE,
                                             bias=ebias[:, m, k, 1:2])
                        ins = nc.scalar.activation(e_one[:, k], score[:, m, k], ACT.Exp,
                                                   bias=ebias[:, m, k, 0:1])
                    ins.then_inc(a_exp, 1)
                if live(1):
                    act.wait_ge(a_W, t)
                    after(act, a_att, t - 3, 0)
                    nc.scalar.activation(
                        wh[:, (ph - 1) % 3, :, 0:D + 1].rearrange("p (b u) f -> p b u f", b=2),
                        psW.rearrange("p b (u f) -> p b u f", u=2), ACT.Copy).then_inc(a_wh, 1)
                if live(3):
                    act.wait_ge(a_PT, t - 2)
                    after(act, a_att, t - 3, 0)
                    for b in range(2):
                        ins = nc.scalar.activation(pT[:, 2 * b:2 * b + 2, :].rearrange("p k i -> p (k i)"),
                                                   psPT[:, b, :], ACT.Copy)
                    ins.then_inc(a_pT, 1)

            act.wait_ge(ones_ok, 1)
            ticks(act, 4, 3, phase_a)

            def phase_b(t, ph, live):
                for s in (4, 3, 2, 1):
                    if not live(s):
                        continue
                    act.wait_ge(b_mm[s], t - s + 1)
                    if s == 4:
                        dst = h_hi[:, bass.ds((t - 4) * PN, PN)]
                    else:
                        dst = s_hi[:, s, :]
                        after(act, b_mm[s + 1], t - s, 0)
                    nc.scalar.activation(dst, ps[:, s, :], ACT.Copy if s in (1, 3) else ACT.Relu).then_inc(b_hi[s], 1)
                if live(0):
                    after(act, b_lo[0], t, 0)
                    normalise(1, t, b_v)

            act.wait_ge(ln_ok, 8)
            ticks(act, 4, 1, phase_b)

            act.wait_ge(wl_ok, 2)
            for p, nb in LSTM:
                nw, cols, its = lstm_shape(p, nb)
                def one(it):
                    def cell_tanh(k, par):
                        act.wait_ge(c_cell[par], it * p + (h_base[p] + k + 1))
                        nc.scalar.activation(lw[:, par, R_TC, 0:cols], lw[:, par, R_C, 0:cols],
                                             ACT.Tanh).then_inc(c_act[par], 1)

                    for k in range(p):
                        for par in range(2):
                            gates = [I, G, O] if k == 0 else [I, G, F, O]
                            g_n = it * gates_of(p) + gate_base[p] + (0 if k == 0 else 3 + 4 * (k - 1))
                            h_n = it * p + h_base[p]
                            for j, g in enumerate(gates):
                                act.wait_ge(c_gate[par], g_n + (j + 1))
                                if k == 0 and j == 0:
                                    after(act, c_h[par], h_n, 0)
                                nc.scalar.activation(lw[:, par, g, 0:cols], ps[:, 4 * par + g, 0:cols],
                                                     ACT.Tanh if g == G else ACT.Sigmoid,
                                                     bias=bl[:, (p - 1) * GATES + g:(p - 1) * GATES + g + 1]
                                                     ).then_inc(c_act[par], 1)
                                if k == 0 and par == 1 and j == 0:
                                    cell_tanh(0, 0)
                            if k > 0 or par == 1:
                                cell_tanh(k, par)
                lstm_rounds(act, p, its, one)

        @block.vector
        def _(dve):
            n = 0

            def done(ins):
                nonlocal n
                n += 1
                ins.then_inc(dve_step, 1)
                dve.wait_ge(dve_step, n)

            for c in range(4):
                dve.wait_ge(x_in[c], 16)
                with dve.Fori(0, QUARTER // 8) as it:
                    for k in range(8):
                        i = it * 8 + (c * QUARTER + k)
                        nc.vector.bn_stats(stats[:, 0, bass.ds(i, 1), :].rearrange("p o s -> p (o s)"),
                                           xs[:, bass.ds(i, 1), :].rearrange("p o f -> p (o f)")
                                           ).then_inc(stats_ok, 1)
                if c == 0:
                    dve.wait_ge(wa_ps, 1)
                    nc.vector.tensor_copy(wext[:, D:D + 1], ps[:, 0, 0:1])
                    nc.vector.tensor_copy(wa2[:, :], ps[:, 0, 1:2].to_broadcast([P, P])).then_inc(wa_ok, 1)
                    dve.wait_ge(adj_in, 32)
                    done(nc.vector.tensor_scalar(adj_neg[:, :, :], adj_raw[:, :, :], 0.0, MASKED, ALU.is_equal,
                                                 ALU.mult))

            base = n

            def phase_a(t, ph, live):
                def statistics(k):
                    if live(5):
                        if k == 0:
                            dve.wait_ge(a_x1, (t - 5) * 2 + 2)
                        i = (t - 5) * 4 + k
                        nc.vector.bn_stats(stats[:, 1, bass.ds(i, 1), :].rearrange("p o s -> p (o s)"),
                                           xs[:, bass.ds(i, 1), :].rearrange("p o f -> p (o f)")
                                           ).then_inc(stats_ok, 1)

                if live(2):
                    m = (ph - 2) % 3
                    a1 = wh[:, m, :, D]
                    dve.wait_ge(a_wh, t - 1)
                    dve.wait_ge(a_t, t - 1)
                    nc.vector.tensor_tensor(vtop[:, :], m2[:, m, :], a1, ALU.add).then_inc(dve_step, 1)
                    statistics(0)
                    dve.wait_ge(dve_step, (t - 2) * 3 + (base + 1))
                    nc.vector.tensor_scalar(vneg[:, :], vtop[:, :], -SLOPE, None, ALU.mult).then_inc(dve_step, 1)
                    statistics(1)
                    dve.wait_ge(dve_step, (t - 2) * 3 + (base + 2))
                    nc.vector.scalar_tensor_tensor(negm[:, :], vtop[:, :], -1.0, vneg[:, :], ALU.mult,
                                                   ALU.min).then_inc(dve_step, 1)
                    statistics(2)
                    dve.wait_ge(dve_step, (t - 2) * 3 + (base + 3))
                    nc.vector.tensor_tensor(ebias[:, m, :, 0], a1, negm[:, :], ALU.add)
                    nc.vector.scalar_tensor_tensor(ebias[:, m, :, 1], a1, SLOPE, negm[:, :], ALU.mult,
                                                   ALU.add).then_inc(a_bias, 1)
                    statistics(3)
                else:
                    for k in range(4):
                        statistics(k)
                if live(4):
                    dve.wait_ge(a_att, t - 3)
                    pa = psA.rearrange("p b (u f) -> p b u f", u=2)
                    nc.vector.reciprocal(rinv[:, :].rearrange("p (b u) -> p b u", b=2),
                                         pa[:, :, :, D + 1]).then_inc(a_x1, 1)
                    dve.wait_ge(a_x1, (t - 4) * 2 + 1)
                    for k in range(4):
                        if k == 3 and live(1):
                            dve.wait_ge(a_S, t)
                        xt = xs[:, bass.ds((t - 4) * 4 + k, 1), :].rearrange("p o f -> p (o f)")
                        ins = nc.vector.scalar_tensor_tensor(xt, pa[:, k // 2, k % 2, 0:D], rinv[:, k:k + 1], xt,
                                                             ALU.mult, ALU.add)
                    ins.then_inc(a_x1, 1)
                if live(1):
                    if not live(4):
                        dve.wait_ge(a_S, t)
                    m = (ph - 1) % 3
                    for k in range(4):
                        b, u = k // 2, k % 2
                        ins = nc.vector.tensor_tensor_reduce(
                            out=score[:, m, k], in0=psS[:, b * N:(b + 1) * N], in1=adj_neg[:, u, :], scale=1.0,
                            scalar=-3e38, op0=ALU.add, op1=ALU.max, accum_out=m2[:, m, k:k + 1])
                    ins.then_inc(a_t, 1)
                if live(2):
                    dve.wait_ge(a_exp, t - 1)
                    after(dve, a_PT, t - 2, 0)
                    nc.vector.tensor_tensor(prob[:, :, :], e_one[:, :, :], e_low[:, :, :],
                                            ALU.max).then_inc(a_P, 1)

            ticks(dve, 5, 3, phase_a)
            n += 3 * PAIRS

            def phase_b(t, ph, live):
                for s in (4, 3, 2, 1):
                    if not live(s):
                        continue
                    dve.wait_ge(b_hi[s], t - s + 1)
                    if s == 4:
                        hi = h_hi[:, bass.ds((t - 4) * PN, PN)]
                        dst = h_lo[:, bass.ds((t - 4) * PN, PN)]
                    else:
                        hi, dst = s_hi[:, s, :], s_lo[:, s, :]
                        after(dve, b_mm[s + 1], t - s, 0)
                    if s in (1, 3):
                        ins = nc.vector.tensor_tensor(dst, ps[:, s, :], hi.bitcast(fp32), ALU.subtract)
                    else:
                        ins = nc.vector.scalar_tensor_tensor(dst, ps[:, s, :], 0.0, hi.bitcast(fp32), ALU.max,
                                                             ALU.subtract)
                    ins.then_inc(b_lo[s], 1)
                if live(0):
                    v = v_norm[:, :, :].rearrange("p k f -> p (k f)")
                    dve.wait_ge(b_v, t + 1)
                    after(dve, b_mm[1], t, 0)
                    nc.vector.tensor_copy(s_hi[:, 0, :], v).then_inc(b_hi[0], 1)
                    dve.wait_ge(b_hi[0], t + 1)
                    nc.vector.tensor_tensor(s_lo[:, 0, :], v, s_hi[:, 0, :].bitcast(fp32),
                                            ALU.subtract).then_inc(b_lo[0], 1)

            dve.wait_ge(rs_ps, 1)
            dve.wait_ge(a_x1, 2 * PAIRS)
            done(nc.vector.tensor_copy(rs_full[:, :].bitcast(fp32r), ps[:, 5, 0:N]))
            nc.vector.tensor_copy(rs_parts[0:64], rs_full[0:64])
            nc.vector.tensor_tensor(rs_parts[64:96], ps[64:96, 5, 0:N], rs_full[64:96], ALU.subtract
                                    ).then_inc(rs_ok, 1)
            ticks(dve, 4, 1, phase_b)

            steps = n
            for p, nb in LSTM:
                nw, cols, its = lstm_shape(p, nb)
                per = sum(2 * ((1 if k == 0 else 3) - 1 + 2) for k in range(p))
                def one(it):
                    s_n = 0
                    for k in range(p):
                        for par in range(2):
                            a_n = it * (gates_of(p) + p) + (act_base[p] + (0 if k == 0 else 4 + 5 * (k - 1)))
                            row = lambda r: lw[:, par, r, 0:cols]

                            def own(ins):
                                nonlocal s_n
                                s_n += 1
                                ins.then_inc(dve_step, 1)
                                dve.wait_ge(dve_step, it * per + (steps + s_n))

                            dve.wait_ge(c_act[par], a_n + 2)
                            if k == 0:
                                nc.vector.tensor_tensor(row(R_C), row(I), row(G), ALU.mult).then_inc(c_cell[par], 1)
                                dve.wait_ge(c_act[par], a_n + 4)
                            else:
                                own(nc.vector.tensor_tensor(row(R_IG), row(I), row(G), ALU.mult))
                                dve.wait_ge(c_act[par], a_n + 3)
                                own(nc.vector.tensor_tensor(row(R_C), row(F), row(R_C), ALU.mult))
                                nc.vector.tensor_tensor(row(R_C), row(R_C), row(R_IG), ALU.add
                                                        ).then_inc(c_cell[par], 1)
                                dve.wait_ge(c_act[par], a_n + 5)
                            own(nc.vector.tensor_tensor(row(R_H), row(O), row(R_TC), ALU.mult))
                            if k == p - 1:
                                hi = window_cols(h_hi, p, nb, it * 2 + par, k)
                                lo = window_cols(h_lo, p, nb, it * 2 + par, k)
                                src = like_cols(lw[:, par, R_H, :], p, nb)
                            else:
                                hi, lo = s_hi[:, par, 0:cols], s_lo[:, par, 0:cols]
                                src = row(R_H)
                            own(nc.vector.tensor_copy(hi, src))
                            nc.vector.tensor_tensor(lo, src, hi.bitcast(fp32), ALU.subtract).then_inc(c_h[par], 1)
                    assert s_n == per
                lstm_rounds(dve, p, its, one)
                steps += its * per

            with dve.Fori(0, PAIRS // 4) as it:
                for par in range(4):
                    q = it * 4 + par
                    dve.wait_ge(d_T, q + 1)
                    xq = xs[:, bass.ds(q * 4, 4), :].rearrange("p k f -> p (k f)")
                    nc.vector.tensor_tensor(xq, ps[:, par, :], xq, ALU.add).then_inc(d_out, 1)

        @block.tensor
        def _(pe):
            pe.wait_ge(gat_w_in, 48)
            nc.tensor.matmul(ps[:, 0, 0:2], wt[:, :], a12[:, :], start=True, stop=True).then_inc(wa_ps, 1)
            pe.wait_ge(ident_ok, 1)
            pe.wait_ge(wa_ok, 1)

            def phase_a(t, ph, live):
                if live(4):
                    pe.wait_ge(a_pT, t - 3)
                    after(pe, a_x1, (t - 4) * 2, 0)
                    for b in range(2):
                        for ui in range(2):
                            for uj in range(2):
                                ins = nc.tensor.matmul(psA[:, b, ui * (D + 2):(ui + 1) * (D + 2)],
                                                       pT[:, 2 * b + uj, ui * P:(ui + 1) * P],
                                                       wh[:, (ph - 4) % 3, 2 * b + uj, :],
                                                       start=(uj == 0), stop=(uj == 1))
                    ins.then_inc(a_att, 1)
                if live(1):
                    pe.wait_ge(a_hT, t)
                    after(pe, a_wh, t - 1, 0)
                    for k in range(4):
                        ins = nc.tensor.matmul(psW[:, k // 2, (k % 2) * (D + 1):(k % 2 + 1) * (D + 1)],
                                               hT[:, k * P:(k + 1) * P], wext[:, :], start=True, stop=True)
                    ins.then_inc(a_W, 1)
                    after(pe, a_t, t - 1, 0)
                    nc.tensor.matmul(psS, wa2[:, :], hT[:, :], start=True, stop=True).then_inc(a_S, 1)
                if live(3):
                    pe.wait_ge(a_P, t - 2)
                    after(pe, a_pT, t - 3, 0)
                    for k in range(4):
                        b, ui = k // 2, k % 2
                        for uj in range(2):
                            ins = nc.tensor.transpose(psPT[:, b, uj * N + ui * P:uj * N + (ui + 1) * P],
                                                      prob[:, k, uj * P:(uj + 1) * P], ident[:, :])
                    ins.then_inc(a_PT, 1)
                if live(0):
                    pe.wait_ge(a_y, t + 1)
                    after(pe, a_hT, t, 0)
                    for k in range(4):
                        ins = nc.tensor.transpose(psT[:, k * P:(k + 1) * P], v_norm[:, k, :], ident[:, :])
                    ins.then_inc(a_T, 1)

            ticks(pe, 4, 3, phase_a)

            def product(dst, w, v, start, stop):
                for n_, (a, b) in enumerate(((w[0], v[0]), (w[1], v[0]), (w[0], v[1]))):
                    ins = nc.tensor.matmul(dst, a, b, start=start and n_ == 0, stop=stop and n_ == 2)
                return ins

            def parts(s):
                return s_hi[:, s, :], s_lo[:, s, :]

            def phase_b(t, ph, live):
                for s in (4, 3, 2, 1):
                    if not live(s):
                        continue
                    after(pe, b_lo[s], t - s, 0)
                    pe.wait_ge(b_lo[s - 1], t - s + 1)
                    hi, lo = parts(s - 1)
                    if s == 2:
                        product(ps[:, s, :], (wg_hi[:, 0, :], wg_lo[:, 0, :]), (hi, lo), True, False)
                        for b in range(2):
                            ins = nc.tensor.matmul(ps[:, s, b * N:(b + 1) * N], b0_parts[:, :], rs_parts[:, :],
                                                   start=False, stop=(b == 1))
                    elif s == 3:
                        nc.tensor.matmul(ps[:, s, :], ones[0:64, :], b1_parts[:, :, :].rearrange("p k f -> p (k f)"),
                                         start=True, stop=False)
                        for k in range(4):
                            c = slice(k * P, (k + 1) * P)
                            ins = product(ps[:, s, c], (hi[:, c], lo[:, c]), (wg_hi[:, 1, :], wg_lo[:, 1, :]),
                                          False, k == 3)
                    else:
                        for b in range(2):
                            for u in range(2):
                                c = slice((2 * b + u) * P, (2 * b + u + 1) * P)
                                ins = product(ps[:, s, b * N:(b + 1) * N], (hi[:, c], lo[:, c]),
                                              (adjT_hi[:, u, :], adjT_lo[:, u, :]), u == 0, u == 1)
                    ins.then_inc(b_mm[s], 1)

            pe.wait_ge(adjT_ok, 1)
            pe.wait_ge(a_pT, PAIRS)
            for j in range(4):
                u, part = j % 2, (adjT_hi, adjT_lo)[j // 2]
                ins = nc.tensor.matmul(ps[:, 5, 0:N], ones[:, :], part[:, u, :], start=(j == 0), stop=(j == 3))
            ins.then_inc(rs_ps, 1)
            pe.wait_ge(b_ok, 1)
            pe.wait_ge(rs_ok, 1)
            ticks(pe, 4, 1, phase_b)

            for s in range(1, 5):
                pe.wait_ge(b_lo[s], PAIRS)
            pe.wait_ge(wl_ok, 2)
            for idx, (p, nb) in enumerate(LSTM):
                nw, cols, its = lstm_shape(p, nb)
                def one(it):
                    for k in range(p):
                        for par in range(2):
                            chunk = it * 2 + par
                            gates = [I, G, O] if k == 0 else [I, G, F, O]
                            if k == 0 and par == 0 and idx > 0:
                                pp, pnb = LSTM[idx - 1]
                                for q in range(2):
                                    pe.wait_ge(c_h[q], it * (pp * nb // pnb) + (h_base[pp] + pp * nb // pnb))
                            a_n = it * (gates_of(p) + p) + act_base[p] + (0 if k == 0 else 5 * k - 2)
                            after(pe, c_act[par], a_n - (1 if k == 0 else 0), 0)
                            w = lambda m, g: (wl_hi[:, m, p - 1, g * D:(g + 1) * D], wl_lo[:, m, p - 1, g * D:(g + 1) * D])
                            v = (window_cols(h_hi, p, nb, chunk, k), window_cols(h_lo, p, nb, chunk, k))
                            dst = lambda g: like_cols(ps[:, 4 * par + g, :], p, nb)
                            for g in gates:
                                ins = product(dst(g), w(0, g), v, True, k == 0)
                                if k == 0:
                                    ins.then_inc(c_gate[par], 1)
                            if k > 0:
                                pe.wait_ge(c_h[par], it * p + (h_base[p] + k))
                                hv = (s_hi[:, par, 0:cols], s_lo[:, par, 0:cols])
                                for g in gates:
                                    product(ps[:, 4 * par + g, 0:cols], w(1, g), hv, False, True
                                            ).then_inc(c_gate[par], 1)
                lstm_rounds(pe, p, its, one)

            pe.wait_ge(c_h[0], h_total)
            pe.wait_ge(c_h[1], h_total)
            for q in range(PAIRS):
                after(pe, d_out, q - 3, 0)
                for k in range(4):
                    c = slice((4 * q + k) * P, (4 * q + k + 1) * P)
                    dst = ps[:, q % 4, k * P:(k + 1) * P]
                    nc.tensor.matmul(dst, h_hi[:, c], ident_r[:, :], start=True, stop=False)
                    ins = nc.tensor.matmul(dst, h_lo[:, c], ident_r[:, :], start=False, stop=True)
                ins.then_inc(d_T, 1)


def kernel(x, adj, L0_gnn_W, L0_gnn_a, L1_gnn_Wg0, L1_gnn_bg0, L1_gnn_Wg1, L1_gnn_bg1, L1_gnn_Wih, L1_gnn_Whh,
           L1_gnn_bih, L1_gnn_bhh):
    import numpy as np
    import concourse.bacc as bacc
    from concourse import mybir
    from concourse.bass_utils import run_bass_kernel_spmd

    x, adj, W = np.asarray(x), np.asarray(adj), np.asarray(L0_gnn_W)
    weight = lambda w: np.ascontiguousarray(np.asarray(w).transpose(2, 0, 1))
    bias = lambda b: np.ascontiguousarray(np.asarray(b).reshape(4, 4, 128).transpose(2, 0, 1))
    ins = {
        "x": x, "adj": adj, "adj_t": np.ascontiguousarray(adj.T), "w_gat": W, "w_gat_t": np.ascontiguousarray(W.T),
        "a_gat": np.ascontiguousarray(np.asarray(L0_gnn_a).reshape(2, 128).T), "w_gcn0": np.asarray(L1_gnn_Wg0), "b_gcn0": np.asarray(L1_gnn_bg0),
        "w_gcn1": np.asarray(L1_gnn_Wg1), "b_gcn1": np.asarray(L1_gnn_bg1), "w_ih_t": weight(L1_gnn_Wih),
        "w_hh_t": weight(L1_gnn_Whh), "b_ih_t": bias(L1_gnn_bih), "b_hh_t": bias(L1_gnn_bhh),
    }
    nc = bacc.Bacc("TRN2", target_bir_lowering=False, num_devices=1)
    arrays, args = {}, []
    for name, a in ins.items():
        arrays[f"in_{name}"] = a
        args.append(nc.dram_tensor(f"in_{name}", a.shape, mybir.dt.from_np(a.dtype), kind="ExternalInput").ap())
    args.append(nc.dram_tensor("result", x.shape, mybir.dt.from_np(x.dtype), kind="ExternalOutput").ap())
    preln_gat_gcn_lstm_kernel(nc, *args)
    r = run_bass_kernel_spmd(nc, [arrays], core_ids=[0])
    return r.results[0]["result"]
```

```python
import concourse.bass as bass
from concourse import mybir
from contextlib import ExitStack


def preln_gat_gcn_lstm_kernel(
    nc: bass.Bass,
    x: bass.AP,
    adj: bass.AP,
    adj_t: bass.AP,
    w_gat: bass.AP,
    w_gat_t: bass.AP,
    a_gat: bass.AP,
    w_gcn0: bass.AP,
    b_gcn0: bass.AP,
    w_gcn1: bass.AP,
    b_gcn1: bass.AP,
    w_ih_t: bass.AP,
    w_hh_t: bass.AP,
    b_ih_t: bass.AP,
    b_hh_t: bass.AP,
    out: bass.AP,
):
    fp32 = mybir.dt.float32
    fp32r = mybir.dt.float32r
    ALU = mybir.AluOpType
    ACT = mybir.ActivationFunctionType

    B, N, D = x.shape
    P = 128
    assert D == P and N == 2 * P
    TILES = B * N // P
    PAIRS = B // 2
    NODES = B * N
    QUARTER = TILES // 4
    X_GROUPS = [(0, 8), (8, 8)] + [(c * QUARTER, QUARTER) for c in range(1, 4)]
    PN = 2 * N
    EPS = 1e-5
    SLOPE = 0.2
    SLOPE_RATIO = SLOPE / (1.0 - SLOPE)
    MASKED = -1e30
    SKIPS = 4
    GCN_LOADS = 10
    GATES = 4
    I, F, G, O = range(GATES)

    x_v = x.rearrange("b (u p) f -> p (b u) f", p=P)
    out_v = out.rearrange("b (u p) f -> p (b u) f", p=P)

    ctx = ExitStack()
    with ctx:
        def sb(name, shape, dt=fp32):
            return ctx.enter_context(nc.sbuf_tensor(name, shape, dt))

        def sem(name):
            return ctx.enter_context(nc.semaphore(name))

        xs = sb("xs", [P, TILES, D])
        wl_hi = sb("wl_hi", [P, 2, SKIPS, GATES * D], fp32r)
        wl_lo = sb("wl_lo", [P, 2, SKIPS, GATES * D], fp32r)
        work = sb("work", [P, 8192])
        s_hi = sb("s_hi", [P, 4, 512], fp32r)
        s_lo = sb("s_lo", [P, 4, 512], fp32r)
        v_norm = sb("v_norm", [P, 4, D])
        adj_raw = sb("adj_raw", [P, 2, N])
        adjT_raw = sb("adjT_raw", [P, 2, N])
        adj_neg = sb("adj_neg", [P, 2, N])
        adjT_hi = sb("adjT_hi", [P, 2, N], fp32r)
        adjT_lo = sb("adjT_lo", [P, 2, N], fp32r)
        wext = sb("wext", [P, D + 1])
        wa2 = sb("wa2", [P, P])
        wt = sb("wt", [P, D])
        a12 = sb("a12", [P, 2])
        wg_raw = sb("wg_raw", [P, 2, D])
        wg_hi = sb("wg_hi", [P, 2, D], fp32r)
        wg_lo = sb("wg_lo", [P, 2, D], fp32r)
        b_raw = sb("b_raw", [96, 2, D])
        b_full = sb("b_full", [96, 2, D])
        b0_parts = sb("b0_parts", [96, D], fp32r)
        b1_parts = sb("b1_parts", [64, 4, D], fp32r)
        rs_full = sb("rs_full", [P, N])
        rs_parts = sb("rs_parts", [96, N], fp32r)
        ones = sb("ones", [P, P], fp32r)
        ident = sb("ident", [P, P])
        ident_r = sb("ident_r", [P, P], fp32r)
        bl_raw = sb("bl_raw", [P, 2, SKIPS * GATES])
        bl = sb("bl", [P, SKIPS * GATES])
        stats = sb("stats", [P, 2, TILES, 6])
        shift = sb("shift", [P, 2, TILES])
        scale = sb("scale", [P, 2, TILES])
        ln_a = sb("ln_a", [P, TILES])
        ln_b = sb("ln_b", [P, TILES])
        ln_c = sb("ln_c", [P, TILES])
        half = sb("half", [P, TILES])
        m2 = sb("m2", [P, 4, 4])
        vtop = sb("vtop", [P, 4])
        vneg = sb("vneg", [P, 4])
        negm = sb("negm", [P, 4])
        ebias = sb("ebias", [P, 4, 4])
        rinv = sb("rinv", [P, 4])

        with ExitStack() as early:
            def sb_early(name, shape):
                return early.enter_context(nc.sbuf_tensor(name, shape, fp32))

            hT = sb_early("hT", [P, 512])
            score = sb_early("score", [P, 4, 4, N])
            prob = sb_early("prob", [P, 4, 4, N])
            pT = sb_early("pT", [P, 4, N])
            wh = sb_early("wh", [P, 4, 4, D + 2])
        h_hi = sb("h_hi", [P, NODES], fp32r)
        with ExitStack() as parts_end:
            h_lo = parts_end.enter_context(nc.sbuf_tensor("h_lo", [P, NODES], fp32r))
        h32 = sb("h32", [P, NODES])

        wraw = work[:, 0:4096].rearrange("p (w s g) -> p w s g", w=2, s=SKIPS)
        lw = work[:, :].rearrange("p (q r n) -> p q r n", q=2, r=8)
        R_C, R_TC, R_IG, R_H = 4, 5, 6, 7

        def one_row(r):
            return lw[:, 1, r, :]

        ps = ctx.enter_context(nc.psum_tensor("ps", [P, 8, 512], fp32))
        psT = ps[:, 0, :]
        psW = ps[:, 1:3, 0:2 * (D + 1)]
        psS = ps[:, 3, :]
        psPT = ps[:, 4:6, :]
        psA = ps[:, 6:8, 0:2 * (D + 2)]

        x_in = [sem(f"x_in{c}") for c in range(len(X_GROUPS))]
        gat_w_in = sem("gat_w_in")
        wext_in = sem("wext_in")
        adj_in = sem("adj_in")
        adjT_in = sem("adjT_in")
        gcn_w_in = sem("gcn_w_in")
        lstm_w_in = sem("lstm_w_in")
        ident_ok = sem("ident_ok")
        pool_step = sem("pool_step")
        b_zero = sem("b_zero")
        ones_ok = sem("ones_ok")
        rs_ps = sem("rs_ps")
        rs_full_ok = sem("rs_full_ok")
        rs_ok = sem("rs_ok")
        adjT_ok = sem("adjT_ok")
        b_ok = sem("b_ok")
        wa_ps = sem("wa_ps")
        wa_ok = sem("wa_ok")
        wl_ok = sem("wl_ok")
        stats_ok = sem("stats_ok")
        ln_ok = sem("ln_ok")
        dve_step = sem("dve_step")
        a_v = sem("a_v")
        a_T = sem("a_T")
        a_hT = sem("a_hT")
        a_W = sem("a_W")
        a_S = sem("a_S")
        a_wh = sem("a_wh")
        a_t = sem("a_t")
        a_bias = sem("a_bias")
        a_exp = sem("a_exp")
        a_z = sem("a_z")
        a_PT = sem("a_PT")
        a_pT = sem("a_pT")
        a_att = sem("a_att")
        a_x1 = sem("a_x1")
        b_v = sem("b_v")
        b_mm = [None] + [sem(f"b_mm{s}") for s in range(1, 5)]
        b_hi = [sem(f"b_hi{s}") for s in range(5)]
        b_lo = [sem(f"b_lo{s}") for s in range(5)]
        one_gate = sem("one_gate")
        one_act = sem("one_act")
        one_cell = sem("one_cell")
        one_h = sem("one_h")
        one_hi = sem("one_hi")
        one_lo = sem("one_lo")
        c_gate = [sem(f"c_gate{q}") for q in range(2)]
        c_act = [sem(f"c_act{q}") for q in range(2)]
        c_h = [sem(f"c_h{q}") for q in range(2)]
        c_ig = [sem(f"c_ig{q}") for q in range(2)]
        c_fc = [sem(f"c_fc{q}") for q in range(2)]
        c_cell = [sem(f"c_cell{q}") for q in range(2)]
        c_hi = [sem(f"c_hi{q}") for q in range(2)]
        c_lo = [sem(f"c_lo{q}") for q in range(2)]
        d_T = sem("d_T")
        d_out = sem("d_out")
        stored = sem("stored")

        BESIDE = 4

        def ticks(eng, depth, unroll, body, first=0, beside=None, lag=0):
            def alive(t):
                return lambda s: 0 <= t - s < PAIRS

            lead = depth + 1 + (PAIRS - depth - 1) % unroll
            for t in range(first, lead):
                body(t, t, alive(t))
            with eng.Fori(0, (PAIRS - lead) // unroll) as it:
                for k in range(unroll):
                    body(it * unroll + (lead + k), lead + k, lambda s: True)
            for t in range(PAIRS, PAIRS + depth):
                body(t, t, alive(t))
                u = t - PAIRS - lag
                if beside and 0 <= u < BESIDE:
                    beside(u, u, alive(u))

        def lstm_rounds(eng, its, body):
            body(0, True)
            with eng.Fori(1, its) as it:
                body(it, False)

        def after(eng, s, n, least=0):
            if not isinstance(n, int) or n > least:
                eng.wait_ge(s, n)

        LSTM = [(2, 4), (3, 4), (4, 8)]

        def lstm_shape(p, nb):
            return N // p, nb * (N // p), B // (2 * nb)

        def gates_of(p):
            return GATES * p - 1

        gate_base, act_base, h_base, fc_base = {}, {}, {}, {}
        g0 = a0 = h0 = f0 = 0
        for p, nb in LSTM:
            gate_base[p], act_base[p], h_base[p], fc_base[p] = g0, a0, h0, f0
            its = lstm_shape(p, nb)[2]
            g0 += its * gates_of(p)
            a0 += its * (gates_of(p) + p)
            h0 += its * p
            f0 += its * (p - 1)
        h_total, a_total = h0, a0

        LAST = LSTM[-1][0]

        def parts_of(p):
            return p - 1 if p == LAST else p

        def count(it, per, base, back=0):
            return it * per + (base - back * per)

        def open_step(idx, it, first):
            if not first:
                return idx, it, 1
            return (idx - 1, lstm_shape(*LSTM[idx - 1])[2], 1) if idx > 0 else None

        def chunk_starts(eng, it, nb, back=0):
            starts = [count(it, 2 * nb * N, par * nb * N, back) for par in range(2)]
            return starts if isinstance(it, int) else [eng.snap(s) for s in starts]

        def window_cols(buf, p, nb, start, k):
            nw = N // p
            v = buf[:, bass.ds(start, nb * N)]
            if N % p == 0:
                return v.rearrange("f (w s) -> f w s", s=p)[:, :, k]
            v = v.rearrange("f (b t) -> f b t", b=nb)[:, :, k:k + (nw - 1) * p + 1:p]
            return v.rearrange("f b w -> f w b")

        def like_cols(buf2d, p, nb):
            nw, cols, _ = lstm_shape(p, nb)
            v = buf2d[:, 0:cols]
            if N % p == 0:
                return v
            return v.rearrange("f (w b) -> f w b", b=nb)

        block = ctx.enter_context(nc.Block())

        @block.sync
        def _(sp):
            for (lo, cnt), arrived in zip(X_GROUPS, x_in):
                sp.dma_start(xs[:, lo:lo + cnt, :], x_v[:, lo:lo + cnt, :]).then_inc(arrived, 16)
            sp.dma_start(wraw[:, 0], w_ih_t).then_inc(lstm_w_in, 16)
            sp.dma_start(wraw[:, 1], w_hh_t).then_inc(lstm_w_in, 16)

            with sp.Fori(0, PAIRS // 2) as q:
                sp.wait_ge(d_out, q * 2 + 1)
                sp.dma_start(out_v[:, bass.ds(q * 8, 4), :], xs[:, bass.ds(q * 8, 4), :]).then_inc(stored, 16)
            sp.wait_ge(stored, 16 * PAIRS)

        @block.gpsimd
        def _(pool):
            n = 0

            def done(ins):
                nonlocal n
                n += 1
                ins.then_inc(pool_step, 1)
                pool.wait_ge(pool_step, n)

            done(nc.gpsimd.memset(b_raw[:, :, :], 0.0))
            nc.gpsimd.nop().then_inc(b_zero, 1)
            done(nc.gpsimd.memset(ident[:, :], 0.0))
            nc.gpsimd.affine_select(out=ident[:, :], in_=ident[:, :], compare_op=ALU.not_equal, fill=1.0, base=0,
                                    pattern=[[-1, P]], channel_multiplier=1).then_inc(ident_ok, 1)
            nc.gpsimd.memset(wh[:, :, :, D + 1:D + 2], 1.0)
            nc.gpsimd.memset(ones[:, :].bitcast(fp32), 1.0).then_inc(ones_ok, 1)
            done(nc.gpsimd.memset(half[:, :], -0.5))

            def norm_scale(which, lo, cnt):
                st = stats[:, which, lo:lo + cnt, :]
                me, qe, mo, qo = st[:, :, 1], st[:, :, 2], st[:, :, 4], st[:, :, 5]
                a, b, d = (v[:, 0:cnt] for v in (ln_a, ln_b, ln_c))
                sc, sh = scale[:, which, lo:lo + cnt], shift[:, which, lo:lo + cnt]
                done(nc.gpsimd.tensor_tensor(b, me, mo, ALU.subtract))
                done(nc.gpsimd.tensor_tensor(d, b, b, ALU.mult))
                done(nc.gpsimd.tensor_scalar(d, d, 0.25, EPS, ALU.mult, ALU.add))
                done(nc.gpsimd.tensor_tensor(b, qe, qo, ALU.add))
                done(nc.gpsimd.tensor_scalar(b, b, 1.0 / D, 0.0, ALU.mult, ALU.add))
                done(nc.gpsimd.tensor_tensor(a, b, d, ALU.add))
                done(nc.gpsimd.tensor_tensor(sc, a, half[:, 0:cnt], ALU.pow))
                done(nc.gpsimd.tensor_tensor(b, me, mo, ALU.add))
                done(nc.gpsimd.tensor_scalar(b, b, -0.5, 0.0, ALU.mult, ALU.add))
                nc.gpsimd.tensor_tensor(sh, b, sc, ALU.mult).then_inc(ln_ok, cnt // 4)
                pool.wait_ge(ln_ok, which * PAIRS + (lo + cnt) // 4)

            for lo, cnt in X_GROUPS:
                pool.wait_ge(stats_ok, lo + cnt)
                norm_scale(0, lo, cnt)

            pool.wait_ge(gcn_w_in, GCN_LOADS * 16)
            done(nc.gpsimd.tensor_copy(wg_hi[:, :, :], wg_raw[:, :, :]))
            nc.gpsimd.tensor_tensor(wg_lo[:, :, :], wg_raw[:, :, :], wg_hi[:, :, :].bitcast(fp32), ALU.subtract)
            nc.gpsimd.tensor_copy(ident_r[:, :], ident[:, :])
            nc.gpsimd.tensor_tensor(bl[:, :], bl_raw[:, 0], bl_raw[:, 1], ALU.add)
            done(nc.gpsimd.tensor_copy(b_full[:, :, :].bitcast(fp32r), b_raw[:, :, :]))
            done(nc.gpsimd.tensor_copy(b0_parts[0:32], b_full[0:32, 0]))
            done(nc.gpsimd.tensor_tensor(b0_parts[32:64], b_raw[32:64, 0], b_full[32:64, 0], ALU.subtract))
            done(nc.gpsimd.tensor_copy(b0_parts[64:96], b_full[64:96, 0]))
            for k in range(4):
                done(nc.gpsimd.tensor_copy(b1_parts[0:32, k], b_full[0:32, 1]))
                done(nc.gpsimd.tensor_tensor(b1_parts[32:64, k], b_raw[32:64, 1], b_full[32:64, 1], ALU.subtract))
            nc.gpsimd.nop().then_inc(b_ok, 1)

            pool.wait_ge(lstm_w_in, 32)
            for w in range(2):
                done(nc.gpsimd.tensor_copy(wl_hi[:, w], wraw[:, w]))
                nc.gpsimd.tensor_tensor(wl_lo[:, w], wraw[:, w], wl_hi[:, w].bitcast(fp32),
                                        ALU.subtract).then_inc(wl_ok, 1)
                pool.wait_ge(wl_ok, w + 1)

            for c in range(4):
                pool.wait_ge(stats_ok, TILES + (c + 1) * QUARTER)
                norm_scale(1, c * QUARTER, QUARTER)

        @block.scalar
        def _(act):
            act.dma_start(wt[:, :], w_gat_t).then_inc(gat_w_in, 16)
            act.dma_start(a12[:, :], a_gat).then_inc(gat_w_in, 16)
            act.dma_start(wext[:, 0:D], w_gat).then_inc(wext_in, 16)
            act.dma_start(adj_raw[:, :, :], adj.rearrange("(u p) n -> p u n", p=P)).then_inc(adj_in, 16)
            act.dma_start(adjT_raw[:, :, :], adj_t.rearrange("(u p) n -> p u n", p=P)).then_inc(adjT_in, 16)
            act.dma_start(wg_raw[:, 0], w_gcn0).then_inc(gcn_w_in, 16)
            act.dma_start(wg_raw[:, 1], w_gcn1).then_inc(gcn_w_in, 16)
            act.dma_start(bl_raw[:, 0], b_ih_t.rearrange("f s g -> f (s g)")).then_inc(gcn_w_in, 16)
            act.dma_start(bl_raw[:, 1], b_hh_t.rearrange("f s g -> f (s g)")).then_inc(gcn_w_in, 16)
            act.wait_ge(b_zero, 1)
            for l, b in enumerate((b_gcn0, b_gcn1)):
                for r in (0, 32, 64):
                    act.dma_start(b_raw[r:r + 1, l, :], b.rearrange("(o f) -> o f", o=1)).then_inc(gcn_w_in, 16)

            def normalise(which, q, which_tiles, s_v):
                for k in which_tiles:
                    i = q * 4 + k
                    ins = nc.scalar.activation(v_norm[:, k, :],
                                               xs[:, bass.ds(i, 1), :].rearrange("p o f -> p (o f)"), ACT.Relu,
                                               scale=scale[:, which, bass.ds(i, 1)],
                                               bias=shift[:, which, bass.ds(i, 1)])
                ins.then_inc(s_v, 1)

            def first_norm(t, ph, live):
                if live(0):
                    if isinstance(t, int):
                        act.wait_ge(ln_ok, t + 1 if t < 6 else PAIRS)
                    after(act, a_T, t, 0)
                    normalise(0, t, range(4), a_v)

            def early_a(t, ph, live):
                if live(1):
                    act.wait_ge(a_W, t)
                    after(act, a_att, t - 4, 0)
                    nc.scalar.activation(
                        wh[:, (ph - 1) % 4, :, 0:D + 1].rearrange("p (b u) f -> p b u f", b=2),
                        psW.rearrange("p b (u f) -> p b u f", u=2), ACT.Copy).then_inc(a_wh, 1)
                if live(0):
                    act.wait_ge(a_T, t + 1)
                    after(act, a_S, t, 0)
                    nc.scalar.activation(hT[:, :], psT, ACT.Relu).then_inc(a_hT, 1)
                if live(2):
                    m = (ph - 2) % 4
                    act.wait_ge(a_bias, t - 1)
                    after(act, a_PT, t - 5, 0)
                    for k in range(4):
                        ins = nc.scalar.activation(prob[:, m, k], score[:, m, k], ACT.Exp, scale=1.0 - SLOPE,
                                                   bias=ebias[:, m, k:k + 1])
                    ins.then_inc(a_exp, 1)

            def late_a(t, ph, live):
                if live(3):
                    act.wait_ge(a_PT, t - 2)
                    after(act, a_att, t - 3, 0)
                    nc.scalar.activation(pT[:, :, :].rearrange("p k i -> p (k i)"),
                                         psPT.rearrange("p b n -> p (b n)"), ACT.Copy).then_inc(a_pT, 1)

            def phase_a(t, ph, live):
                behind = (t - 1, ph - 1, lambda s: live(s + 1))
                early_a(*behind)
                first_norm(t, ph, live)
                late_a(*behind)

            act.wait_ge(ones_ok, 1)
            def phase_b(t, ph, live):
                if live(6):
                    act.wait_ge(one_cell, t - 5)
                    nc.scalar.activation(one_row(R_TC), one_row(R_C), ACT.Tanh).then_inc(one_act, 1)
                if live(5):
                    for j, g in enumerate((I, G, O)):
                        act.wait_ge(one_gate, t * 3 + (j + 1 - 15))
                        if g == O:
                            after(act, one_h, t - 5, 0)
                        nc.scalar.activation(one_row(g), ps[:, 4 + g, :], ACT.Tanh if g == G else ACT.Sigmoid,
                                             bias=bl[:, g:g + 1]).then_inc(one_act, 1)
                for s in (4, 3, 2, 1):
                    if not live(s):
                        continue
                    act.wait_ge(b_mm[s], t - s + 1)
                    if s == 4:
                        dst = h_hi[:, bass.ds((t - 4) * PN, PN)]
                    else:
                        dst = s_hi[:, s, :]
                        after(act, b_mm[s + 1], t - s, 0)
                    nc.scalar.activation(dst, ps[:, s - 1, :], ACT.Copy if s in (1, 3) else ACT.Relu).then_inc(b_hi[s], 1)
                if live(0):
                    after(act, b_lo[0], t, 0)
                    if isinstance(t, int) and t == 0:
                        act.wait_ge(a_T, PAIRS)
                    act.wait_ge(ln_ok, t + (PAIRS + 1))
                    normalise(1, t, range(4), b_v)

            ticks(act, 5, 4, phase_a, beside=phase_b, lag=1)
            ticks(act, 6, 1, phase_b, first=BESIDE)

            act.wait_ge(wl_ok, 2)

            def cell_tanh(idx, it, back, k, par):
                p, nb = LSTM[idx]
                cols = lstm_shape(p, nb)[1]
                act.wait_ge(c_cell[par], count(it, p, h_base[p] + k + 1, back))
                nc.scalar.activation(lw[:, par, R_TC, 0:cols], lw[:, par, R_C, 0:cols], ACT.Tanh
                                     ).then_inc(c_act[par], 1)

            for idx, (p, nb) in enumerate(LSTM):
                nw, cols, its = lstm_shape(p, nb)

                def one(it, first):
                    def gate(k, par, g):
                        j = ([I, G, O] if k == 0 else [I, G, F, O]).index(g)
                        before = 0 if k == 0 else 3 + 4 * (k - 1)
                        act.wait_ge(c_gate[par], count(it, gates_of(p), gate_base[p] + before + j + 1))
                        if k == 0 and g == O:
                            after(act, c_h[par], count(it, p, h_base[p]), 0)
                        nc.scalar.activation(lw[:, par, g, 0:cols], ps[:, 4 * par + g, 0:cols],
                                             ACT.Tanh if g == G else ACT.Sigmoid,
                                             bias=bl[:, (p - 1) * GATES + g:(p - 1) * GATES + g + 1]
                                             ).then_inc(c_act[par], 1)

                    for g in (I, G, O):
                        gate(0, 0, g)
                    cell_tanh(idx, it, 0, 0, 0)
                    if open_step(idx, it, first):
                        q_idx, q_it, back = open_step(idx, it, first)
                        cell_tanh(q_idx, q_it, back, LSTM[q_idx][0] - 1, 1)
                    if first and idx == 0:
                        act.wait_ge(one_h, PAIRS)
                    for g in (I, G, O):
                        gate(0, 1, g)
                    cell_tanh(idx, it, 0, 0, 1)
                    for k in range(1, p):
                        for par in range(2):
                            for g in (I, G, F, O):
                                gate(k, par, g)
                            if (k, par) != (p - 1, 1):
                                cell_tanh(idx, it, 0, k, par)

                lstm_rounds(act, its, one)
            p, nb = LSTM[-1]
            cell_tanh(len(LSTM) - 1, lstm_shape(p, nb)[2], 1, p - 1, 1)

            with act.Fori(0, PAIRS // 2) as q:
                act.wait_ge(d_out, q * 2 + 2)
                act.dma_start(out_v[:, bass.ds(q * 8 + 4, 4), :], xs[:, bass.ds(q * 8 + 4, 4), :]).then_inc(stored, 16)

        @block.vector
        def _(dve):
            n = 0

            def done(ins):
                nonlocal n
                n += 1
                ins.then_inc(dve_step, 1)
                dve.wait_ge(dve_step, n)

            def first_statistics(c, part):
                dve.wait_ge(x_in[c], 16)
                for k in range(8):
                    i = X_GROUPS[c][0] + part * 8 + k
                    nc.vector.bn_stats(stats[:, 0, i, :], xs[:, i, :]).then_inc(stats_ok, 1)

            first_statistics(0, 0)
            first_statistics(1, 0)
            dve.wait_ge(wa_ps, 1)
            nc.vector.tensor_scalar(wext[:, D:D + 1], ps[:, 0, 0:1], -1.0, None, ALU.mult)
            nc.vector.tensor_copy(wa2[:, :], ps[:, 0, 1:2].to_broadcast([P, P])).then_inc(wa_ok, 1)
            first_statistics(2, 0)
            dve.wait_ge(adj_in, 16)
            done(nc.vector.tensor_scalar(adj_neg[:, :, :], adj_raw[:, :, :], 0.0, MASKED, ALU.is_equal, ALU.mult))

            def adj_parts():
                dve.wait_ge(adjT_in, 16)
                done(nc.vector.tensor_copy(adjT_hi[:, :, :], adjT_raw[:, :, :]))
                nc.vector.tensor_tensor(adjT_lo[:, :, :], adjT_raw[:, :, :], adjT_hi[:, :, :].bitcast(fp32),
                                        ALU.subtract).then_inc(adjT_ok, 1)

            def row_sum_parts():
                dve.wait_ge(rs_ps, 1)
                nc.vector.tensor_copy(rs_full[:, :].bitcast(fp32r), ps[:, 7, 0:N]).then_inc(rs_full_ok, 1)
                dve.wait_ge(rs_full_ok, 1)
                nc.vector.tensor_copy(rs_parts[0:64], rs_full[0:64])
                nc.vector.tensor_tensor(rs_parts[64:96], ps[64:96, 7, 0:N], rs_full[64:96], ALU.subtract
                                        ).then_inc(rs_ok, 1)

            base = n + 1

            def phase_a(t, ph, live):
                def statistics(k):
                    if live(5):
                        if k == 0:
                            dve.wait_ge(a_x1, (t - 5) * 2 + 2)
                        i = (t - 5) * 4 + k
                        nc.vector.bn_stats(stats[:, 1, bass.ds(i, 1), :].rearrange("p o s -> p (o s)"),
                                           xs[:, bass.ds(i, 1), :].rearrange("p o f -> p (o f)")
                                           ).then_inc(stats_ok, 1)

                def scores(k):
                    b, u, m = k // 2, k % 2, (ph - 1) % 4
                    return nc.vector.tensor_tensor_reduce(
                        out=score[:, m, k], in0=psS[:, b * N:(b + 1) * N], in1=adj_neg[:, u, :],
                        scale=SLOPE_RATIO, scalar=-3e38, op0=ALU.add, op1=ALU.max, accum_out=m2[:, m, k:k + 1])

                def row_maximum(k):
                    m = (ph - 2) % 4
                    minus_a1 = wh[:, m, :, D]
                    if k:
                        dve.wait_ge(dve_step, (t - 2) * 3 + (base + k))
                    if k == 0:
                        nc.vector.scalar_tensor_tensor(vtop[:, :], m2[:, m, :], 1.0 / SLOPE_RATIO, minus_a1, ALU.mult,
                                                       ALU.subtract).then_inc(dve_step, 1)
                    elif k == 1:
                        nc.vector.tensor_scalar(vneg[:, :], vtop[:, :], -SLOPE, None, ALU.mult).then_inc(dve_step, 1)
                    elif k == 2:
                        nc.vector.scalar_tensor_tensor(negm[:, :], vtop[:, :], -1.0, vneg[:, :], ALU.mult,
                                                       ALU.min).then_inc(dve_step, 1)
                    else:
                        nc.vector.tensor_tensor(ebias[:, m, :], negm[:, :], minus_a1, ALU.subtract
                                                ).then_inc(a_bias, 1)

                if live(1):
                    dve.wait_ge(a_S, t)
                for k in range(4):
                    if live(2):
                        row_maximum(k)
                    if live(1):
                        ins = scores(k)
                if live(1):
                    ins.then_inc(a_t, 1)
                for k in range(2):
                    statistics(k)
                if live(1):
                    dve.wait_ge(a_wh, t)
                    dve.wait_ge(a_t, t)
                    for k in range(4):
                        m, b = (ph - 1) % 4, k // 2
                        ins = nc.vector.scalar_tensor_tensor(score[:, m, k], psS[:, b * N:(b + 1) * N],
                                                             wh[:, m, k, D:D + 1], score[:, m, k], ALU.max, ALU.add)
                    ins.then_inc(a_z, 1)
                if live(4):
                    dve.wait_ge(a_att, t - 3)
                    pa = psA.rearrange("p b (u f) -> p b u f", u=2)
                    nc.vector.reciprocal(rinv[:, :].rearrange("p (b u) -> p b u", b=2),
                                         pa[:, :, :, D + 1]).then_inc(a_x1, 1)
                    for k in range(2, 4):
                        statistics(k)
                    dve.wait_ge(a_x1, (t - 4) * 2 + 1)
                    for k in range(4):
                        xt = xs[:, bass.ds((t - 4) * 4 + k, 1), :].rearrange("p o f -> p (o f)")
                        ins = nc.vector.scalar_tensor_tensor(xt, pa[:, k // 2, k % 2, 0:D], rinv[:, k:k + 1], xt,
                                                             ALU.mult, ALU.add)
                    ins.then_inc(a_x1, 1)
                else:
                    for k in range(2, 4):
                        statistics(k)
                if isinstance(t, int) and t == 1:
                    adj_parts()
                if isinstance(t, int) and t == 3:
                    row_sum_parts()
                if isinstance(t, int) and t < 5:
                    first_statistics((t + 5) // 2, (t + 1) % 2)

            def phase_b(t, ph, live):
                if live(6):
                    hi, lo = (h[:, bass.ds((t - 6) * PN, PN)] for h in (h_hi, h_lo))
                    dve.wait_ge(one_act, t * 4 - 20)
                    after(dve, one_lo, t - 6, 0)
                    nc.vector.tensor_tensor(one_row(R_H), one_row(O), one_row(R_TC), ALU.mult).then_inc(one_h, 1)
                    dve.wait_ge(one_h, t - 5)
                    nc.vector.tensor_copy(hi, one_row(R_H)).then_inc(one_hi, 1)
                if live(5):
                    dve.wait_ge(one_act, t * 4 - 18)
                    nc.vector.tensor_tensor(one_row(R_C), one_row(I), one_row(G), ALU.mult).then_inc(one_cell, 1)
                if live(6):
                    dve.wait_ge(one_hi, t - 5)
                    nc.vector.tensor_tensor(lo, one_row(R_H), hi.bitcast(fp32), ALU.subtract).then_inc(one_lo, 1)
                for s in (4, 3, 2, 1):
                    if not live(s):
                        continue
                    dve.wait_ge(b_hi[s], t - s + 1)
                    if s == 4:
                        hi = h_hi[:, bass.ds((t - 4) * PN, PN)]
                        dst = h_lo[:, bass.ds((t - 4) * PN, PN)]
                    else:
                        hi, dst = s_hi[:, s, :], s_lo[:, s, :]
                        after(dve, b_mm[s + 1], t - s, 0)
                    if s in (1, 3):
                        ins = nc.vector.tensor_tensor(dst, ps[:, s - 1, :], hi.bitcast(fp32), ALU.subtract)
                    else:
                        ins = nc.vector.scalar_tensor_tensor(dst, ps[:, s - 1, :], 0.0, hi.bitcast(fp32), ALU.max,
                                                             ALU.subtract)
                    ins.then_inc(b_lo[s], 1)
                if live(0):
                    v = v_norm[:, :, :].rearrange("p k f -> p (k f)")
                    dve.wait_ge(b_v, t + 1)
                    after(dve, b_mm[1], t, 0)
                    nc.vector.tensor_copy(s_hi[:, 0, :], v).then_inc(b_hi[0], 1)
                    dve.wait_ge(b_hi[0], t + 1)
                    nc.vector.tensor_tensor(s_lo[:, 0, :], v, s_hi[:, 0, :].bitcast(fp32),
                                            ALU.subtract).then_inc(b_lo[0], 1)

            ticks(dve, 5, 4, phase_a, beside=phase_b)
            ticks(dve, 6, 1, phase_b, first=BESIDE)

            def row(par, r, cols):
                return lw[:, par, r, 0:cols]

            def acts(idx, it, back, par, k, n_):
                p = LSTM[idx][0]
                before = 0 if k == 0 else 4 + 5 * (k - 1)
                dve.wait_ge(c_act[par], count(it, gates_of(p) + p, act_base[p] + before + n_, back))

            def places(idx, starts, par, k):
                p, nb = LSTM[idx]
                cols = lstm_shape(p, nb)[1]
                if k < p - 1:
                    return s_hi[:, par, 0:cols], s_lo[:, par, 0:cols], lambda v: v[:, 0:cols]
                return (window_cols(h_hi, p, nb, starts[par], k), window_cols(h_lo, p, nb, starts[par], k),
                        lambda v: like_cols(v, p, nb))

            def part_hi(idx, it, back, starts, k, par):
                hi, lo, shaped = places(idx, starts, par, k)
                acts(idx, it, back, par, k, 4 if k == 0 else 5)
                nc.vector.tensor_tensor(hi, shaped(lw[:, par, O, :]), shaped(lw[:, par, R_TC, :]), ALU.mult
                                        ).then_inc(c_hi[par], 1)

            def full_h(idx, it, back, k, par):
                cols = lstm_shape(*LSTM[idx])[1]
                nc.vector.tensor_tensor(row(par, R_H, cols), row(par, O, cols), row(par, R_TC, cols), ALU.mult
                                        ).then_inc(c_h[par], 1)

            def part_lo(idx, it, back, starts, k, par):
                p = LSTM[idx][0]
                hi, lo, shaped = places(idx, starts, par, k)
                dve.wait_ge(c_hi[par], count(it, parts_of(p), h_base[p] + k + 1, back))
                dve.wait_ge(c_h[par], count(it, p, h_base[p] + k + 1, back))
                nc.vector.tensor_tensor(lo, shaped(lw[:, par, R_H, :]), hi.bitcast(fp32), ALU.subtract
                                        ).then_inc(c_lo[par], 1)

            def result_h(idx, it, back, starts, par):
                p, nb = LSTM[idx]
                acts(idx, it, back, par, p - 1, 5)
                nc.vector.tensor_tensor(window_cols(h32, p, nb, starts[par], p - 1),
                                        lw[:, par, O, 0:lstm_shape(p, nb)[1]],
                                        lw[:, par, R_TC, 0:lstm_shape(p, nb)[1]], ALU.mult).then_inc(c_h[par], 1)

            def join(idx, starts, k, par):
                p, nb = LSTM[idx]
                hi, lo = (window_cols(h, p, nb, starts[par], k).bitcast(fp32) for h in (h_hi, h_lo))
                nc.vector.tensor_tensor(window_cols(h32, p, nb, starts[par], k), hi, lo, ALU.add)

            def cell(idx, it, k, par):
                p, nb = LSTM[idx]
                cols = lstm_shape(p, nb)[1]
                c, ig = row(par, R_C, cols), row(par, R_IG, cols)
                acts(idx, it, 0, par, k, 2)
                if k == 0:
                    nc.vector.tensor_tensor(c, row(par, I, cols), row(par, G, cols), ALU.mult
                                            ).then_inc(c_cell[par], 1)
                    return
                nc.vector.tensor_tensor(ig, row(par, I, cols), row(par, G, cols), ALU.mult).then_inc(c_ig[par], 1)
                acts(idx, it, 0, par, k, 3)
                nc.vector.tensor_tensor(c, row(par, F, cols), c, ALU.mult).then_inc(c_fc[par], 1)
                if (k, par) != (p - 1, 1):
                    cell_sum(idx, it, 0, k, par)

            def cell_sum(idx, it, back, k, par):
                p, nb = LSTM[idx]
                cols = lstm_shape(p, nb)[1]
                c, ig = row(par, R_C, cols), row(par, R_IG, cols)
                m = count(it, p - 1, fc_base[p] + k, back)
                dve.wait_ge(c_ig[par], m)
                dve.wait_ge(c_fc[par], m)
                nc.vector.tensor_tensor(c, c, ig, ALU.add).then_inc(c_cell[par], 1)

            for idx, (p, nb) in enumerate(LSTM):
                nw, cols, its = lstm_shape(p, nb)

                def one(it, first):
                    starts = chunk_starts(dve, it, nb)
                    cell(idx, it, 0, 0)
                    pend = open_step(idx, it, first)
                    if pend:
                        q_idx, q_it, back = pend
                        q_p, q_nb = LSTM[q_idx]
                        prev = chunk_starts(dve, q_it, q_nb, 1)
                        cell_sum(q_idx, q_it, back, q_p - 1, 1)
                    part_hi(idx, it, 0, starts, 0, 0)
                    full_h(idx, it, 0, 0, 0)
                    if pend and q_p == LAST:
                        result_h(q_idx, q_it, back, prev, 1)
                    elif pend:
                        part_hi(q_idx, q_it, back, prev, q_p - 1, 1)
                        full_h(q_idx, q_it, back, q_p - 1, 1)
                    part_lo(idx, it, 0, starts, 0, 0)
                    if pend and q_p < LAST:
                        part_lo(q_idx, q_it, back, prev, q_p - 1, 1)
                    for k in range(p):
                        for par in range(2):
                            if (k, par) == (0, 0):
                                continue
                            cell(idx, it, k, par)
                            if p == LAST and k > 0:
                                join(idx, starts, k - 1, par)
                            if (k, par) == (LAST - 1, 0):
                                result_h(idx, it, 0, starts, par)
                            elif (k, par) != (p - 1, 1):
                                part_hi(idx, it, 0, starts, k, par)
                                full_h(idx, it, 0, k, par)
                                part_lo(idx, it, 0, starts, k, par)

                lstm_rounds(dve, its, one)

            def add_pair(q, bank):
                dve.wait_ge(d_T, q + 1)
                xq = xs[:, bass.ds(q * 4, 4), :].rearrange("p k f -> p (k f)")
                nc.vector.tensor_tensor(xq, ps[:, bank, :], xq, ALU.add).then_inc(d_out, 1)

            cell_sum(idx, its, 1, p - 1, 1)
            for q in range(4):
                add_pair(q, q)
                if q == 1:
                    result_h(idx, its, 1, chunk_starts(dve, its, nb, 1), 1)
            with dve.Fori(1, PAIRS // 4) as it:
                for bank in range(4):
                    add_pair(it * 4 + bank, bank)

        @block.tensor
        def _(pe):
            pe.wait_ge(gat_w_in, 32)
            nc.tensor.matmul(ps[:, 0, 0:2], wt[:, :], a12[:, :], start=True, stop=True).then_inc(wa_ps, 1)
            pe.wait_ge(ident_ok, 1)
            pe.wait_ge(wa_ok, 1)
            pe.wait_ge(wext_in, 16)

            def adj_row_sums():
                pe.wait_ge(ones_ok, 1)
                pe.wait_ge(adjT_ok, 1)
                for j in range(4):
                    u, part = j % 2, (adjT_hi, adjT_lo)[j // 2]
                    ins = nc.tensor.matmul(ps[:, 7, 0:N], ones[:, :], part[:, u, :], start=(j == 0), stop=(j == 3))
                ins.then_inc(rs_ps, 1)

            def phase_a(t, ph, live):
                if isinstance(t, int) and t == 3:
                    adj_row_sums()
                if isinstance(t, int) and t == 4:
                    pe.wait_ge(rs_ok, 1)
                if live(1):
                    pe.wait_ge(a_hT, t)
                    after(pe, a_wh, t - 1, 0)
                    for k in range(4):
                        ins = nc.tensor.matmul(psW[:, k // 2, (k % 2) * (D + 1):(k % 2 + 1) * (D + 1)],
                                               hT[:, k * P:(k + 1) * P], wext[:, :], start=True, stop=True)
                    ins.then_inc(a_W, 1)
                    after(pe, a_z, t - 1, 0)
                    nc.tensor.matmul(psS, wa2[:, :], hT[:, :], start=True, stop=True).then_inc(a_S, 1)
                if live(0):
                    pe.wait_ge(a_v, t + 1)
                    after(pe, a_hT, t, 0)
                    for k in range(4):
                        ins = nc.tensor.transpose(psT[:, k * P:(k + 1) * P], v_norm[:, k, :], ident[:, :])
                    ins.then_inc(a_T, 1)
                if live(4):
                    pe.wait_ge(a_pT, t - 3)
                    after(pe, a_x1, (t - 4) * 2, 0)
                    for b in range(2):
                        for ui in range(2):
                            for uj in range(2):
                                ins = nc.tensor.matmul(psA[:, b, ui * (D + 2):(ui + 1) * (D + 2)],
                                                       pT[:, 2 * b + uj, ui * P:(ui + 1) * P],
                                                       wh[:, (ph - 4) % 4, 2 * b + uj, :],
                                                       start=(uj == 0), stop=(uj == 1))
                    ins.then_inc(a_att, 1)
                if live(3):
                    pe.wait_ge(a_exp, t - 2)
                    after(pe, a_pT, t - 3, 0)
                    for k in range(4):
                        b, ui = k // 2, k % 2
                        for uj in range(2):
                            ins = nc.tensor.transpose(psPT[:, b, uj * N + ui * P:uj * N + (ui + 1) * P],
                                                      prob[:, (ph - 3) % 4, k, uj * P:(uj + 1) * P], ident[:, :])
                    ins.then_inc(a_PT, 1)

            def product(dst, w, v, start, stop):
                for n_, (a, b) in enumerate(((w[0], v[0]), (w[1], v[0]), (w[0], v[1]))):
                    ins = nc.tensor.matmul(dst, a, b, start=start and n_ == 0, stop=stop and n_ == 2)
                return ins

            def parts(s):
                return s_hi[:, s, :], s_lo[:, s, :]

            def phase_b(t, ph, live):
                if live(5):
                    if isinstance(t, int) and t == 5:
                        pe.wait_ge(a_pT, PAIRS)
                        pe.wait_ge(a_x1, 2 * PAIRS)
                        pe.wait_ge(wl_ok, 2)
                    pe.wait_ge(b_lo[4], t - 4)
                    after(pe, one_act, t * 4 - 21, 0)
                    c = bass.ds((t - 5) * PN, PN)
                    for g in (I, G, O):
                        w = slice(g * D, (g + 1) * D)
                        product(ps[:, 4 + g, :], (wl_hi[:, 0, 0, w], wl_lo[:, 0, 0, w]), (h_hi[:, c], h_lo[:, c]),
                                True, True).then_inc(one_gate, 1)
                for s in (4, 3, 2, 1):
                    if not live(s):
                        continue
                    after(pe, b_lo[s], t - s, 0)
                    if isinstance(t, int) and t == s:
                        pe.wait_ge((a_hT, a_wh, a_wh, a_z)[s - 1], PAIRS)
                    pe.wait_ge(b_lo[s - 1], t - s + 1)
                    hi, lo = parts(s - 1)
                    if isinstance(t, int) and t == 2 and s == 2:
                        pe.wait_ge(b_ok, 1)
                    if s == 2:
                        product(ps[:, s - 1, :], (wg_hi[:, 0, :], wg_lo[:, 0, :]), (hi, lo), True, False)
                        for b in range(2):
                            ins = nc.tensor.matmul(ps[:, s - 1, b * N:(b + 1) * N], b0_parts[:, :], rs_parts[:, :],
                                                   start=False, stop=(b == 1))
                    elif s == 3:
                        nc.tensor.matmul(ps[:, s - 1, :], ones[0:64, :], b1_parts[:, :, :].rearrange("p k f -> p (k f)"),
                                         start=True, stop=False)
                        for k in range(4):
                            c = slice(k * P, (k + 1) * P)
                            ins = product(ps[:, s - 1, c], (hi[:, c], lo[:, c]), (wg_hi[:, 1, :], wg_lo[:, 1, :]),
                                          False, k == 3)
                    else:
                        for b in range(2):
                            for u in range(2):
                                c = slice((2 * b + u) * P, (2 * b + u + 1) * P)
                                ins = product(ps[:, s - 1, b * N:(b + 1) * N], (hi[:, c], lo[:, c]),
                                              (adjT_hi[:, u, :], adjT_lo[:, u, :]), u == 0, u == 1)
                    ins.then_inc(b_mm[s], 1)

            ticks(pe, 4, 4, phase_a, beside=phase_b)
            ticks(pe, 6, 1, phase_b, first=BESIDE)

            for idx, (p, nb) in enumerate(LSTM):
                nw, cols, its = lstm_shape(p, nb)

                def one(it, first):
                    starts = chunk_starts(pe, it, nb)
                    for k in range(p):
                        for par in range(2):
                            gates = [I, G, O] if k == 0 else [I, G, F, O]
                            if first and idx == 0 and k == 0:
                                if par == 0:
                                    for s in range(1, 5):
                                        pe.wait_ge(b_lo[s], PAIRS)
                                else:
                                    pe.wait_ge(one_act, 4 * PAIRS - 1)
                            if k == 0 and par == 0 and idx == 0:
                                pe.wait_ge(one_lo, it * nb + nb)
                            if k == 0 and par == 0 and idx > 0:
                                pp, pnb = LSTM[idx - 1]
                                for q in range(2):
                                    pe.wait_ge(c_lo[q], it * (pp * nb // pnb) + (h_base[pp] + pp * nb // pnb))
                            a_n = count(it, gates_of(p) + p, act_base[p] + (0 if k == 0 else 5 * k - 1))
                            if k == 0:
                                seen = [I, G, F, O]
                            else:
                                seen = [I, G, O] if k == 1 else [I, G, F, O]

                            def w(m, g):
                                c = slice(g * D, (g + 1) * D)
                                return wl_hi[:, m, p - 1, c], wl_lo[:, m, p - 1, c]

                            v = (window_cols(h_hi, p, nb, starts[par], k), window_cols(h_lo, p, nb, starts[par], k))
                            for g in gates:
                                if g in seen:
                                    after(pe, c_act[par], a_n - (len(seen) - seen.index(g)), 0)
                                ins = product(like_cols(ps[:, 4 * par + g, :], p, nb), w(0, g), v, True, k == 0)
                                if k == 0:
                                    ins.then_inc(c_gate[par], 1)
                            if k > 0:
                                h_n = it * parts_of(p) + (h_base[p] + k)
                                pe.wait_ge(c_hi[par], h_n)
                                for g in gates:
                                    for part in w(1, g):
                                        nc.tensor.matmul(ps[:, 4 * par + g, 0:cols], part, s_hi[:, par, 0:cols],
                                                         start=False, stop=False)
                                pe.wait_ge(c_lo[par], h_n)
                                for g in gates:
                                    nc.tensor.matmul(ps[:, 4 * par + g, 0:cols], w(1, g)[0], s_lo[:, par, 0:cols],
                                                     start=False, stop=True).then_inc(c_gate[par], 1)

                lstm_rounds(pe, its, one)

            last_chunk = PAIRS - LSTM[-1][1] // 2
            for q in range(PAIRS):
                if q == 0:
                    for par in range(2):
                        pe.wait_ge(c_h[par], h_total - LAST)
                    pe.wait_ge(c_act[0], a_total - 1)
                if q == last_chunk - LSTM[-1][1] // 2:
                    pe.wait_ge(c_h[0], h_total)
                if q == last_chunk:
                    pe.wait_ge(c_h[1], h_total)
                after(pe, d_out, q - 3, 0)
                for k in range(4):
                    c = slice((4 * q + k) * P, (4 * q + k + 1) * P)
                    ins = nc.tensor.transpose(ps[:, q % 4, k * P:(k + 1) * P], h32[:, c], ident[:, :])
                ins.then_inc(d_T, 1)


def kernel(x, adj, L0_gnn_W, L0_gnn_a, L1_gnn_Wg0, L1_gnn_bg0, L1_gnn_Wg1, L1_gnn_bg1, L1_gnn_Wih, L1_gnn_Whh,
           L1_gnn_bih, L1_gnn_bhh):
    import numpy as np
    import concourse.bacc as bacc
    from concourse import mybir
    from concourse.bass_utils import run_bass_kernel_spmd

    x, adj, W = np.asarray(x), np.asarray(adj), np.asarray(L0_gnn_W)
    weight = lambda w: np.ascontiguousarray(np.asarray(w).transpose(2, 0, 1))
    bias = lambda b: np.ascontiguousarray(np.asarray(b).reshape(4, 4, 128).transpose(2, 0, 1))
    ins = {
        "x": x, "adj": adj, "adj_t": np.ascontiguousarray(adj.T), "w_gat": W, "w_gat_t": np.ascontiguousarray(W.T),
        "a_gat": np.ascontiguousarray(np.asarray(L0_gnn_a).reshape(2, 128).T), "w_gcn0": np.asarray(L1_gnn_Wg0), "b_gcn0": np.asarray(L1_gnn_bg0),
        "w_gcn1": np.asarray(L1_gnn_Wg1), "b_gcn1": np.asarray(L1_gnn_bg1), "w_ih_t": weight(L1_gnn_Wih),
        "w_hh_t": weight(L1_gnn_Whh), "b_ih_t": bias(L1_gnn_bih), "b_hh_t": bias(L1_gnn_bhh),
    }
    nc = bacc.Bacc("TRN2", target_bir_lowering=False, num_devices=1)
    arrays, args = {}, []
    for name, a in ins.items():
        arrays[f"in_{name}"] = a
        args.append(nc.dram_tensor(f"in_{name}", a.shape, mybir.dt.from_np(a.dtype), kind="ExternalInput").ap())
    args.append(nc.dram_tensor("result", x.shape, mybir.dt.from_np(x.dtype), kind="ExternalOutput").ap())
    preln_gat_gcn_lstm_kernel(nc, *args)
    r = run_bass_kernel_spmd(nc, [arrays], core_ids=[0])
    return r.results[0]["result"]
```
